# Optimizing a Trainium2 kernel written in Bass

```python
import numpy as np
import jax
import jax.numpy as jnp

def _softmax(x, axis=-1):
    return jax.nn.softmax(x, axis=axis)

def _gelu(x):
    return jax.nn.gelu(x, approximate=True)

def _silu(x):
    return jax.nn.silu(x)

def _sigmoid(x):
    return jax.nn.sigmoid(x)

def _layernorm(x, axis=-1, eps=1e-05):
    m = jnp.mean(x, axis=axis, keepdims=True)
    v = jnp.var(x, axis=axis, keepdims=True)
    return (x - m) / jnp.sqrt(v + eps)

def _scatter_add(tgt, idx, src, axis=0):
    return tgt.at[idx].add(src)

def _segment_sum(src, seg, n):
    return jax.ops.segment_sum(src, seg, n)
kernel_name = 'mk_adj_resnorm_d2_adj_r2_9b6c32'

def setup_inputs(seed: int=0):
    np.random.seed(seed)
    _w = jnp.asarray

    def _rec_inputs():
        import jax
        import jax.numpy as jnp
        _gk = jax.random.key(seed)
        x = 7.22e-05 + 1 * jax.random.normal(jax.random.fold_in(_gk, 1), (32, 256, 256), jnp.float32)
        _a = jax.random.bernoulli(jax.random.fold_in(_gk, 2), 0.0625, (32, 256, 256))
        _a = jnp.logical_or(_a, jnp.eye(256, dtype=bool))
        _af = _a.astype(jnp.float32)
        _af = _af * jax.random.uniform(jax.random.fold_in(_gk, 3), (32, 256, 256), jnp.float32, 0.05, 1)
        adj = _af
        return (x, adj)
    x, adj = _rec_inputs()

    def _L0_gnn_setup():
        import jax, jax.numpy as jnp
        import numpy as np
        B, N, D_IN, D_OUT = (4, 2048, 256, 256)
        key = jax.random.key(seed)
        k1, k2, k3, k4 = jax.random.split(key, 4)
        x = jax.random.normal(k1, (B, N, D_IN), dtype=jnp.float32)
        A_shape = jax.random.uniform(k2, (B, N, N), dtype=jnp.float32)
        w = jax.random.normal(k3, (D_IN, D_OUT), dtype=jnp.float32)
        a = jax.random.normal(k4, (D_OUT,), dtype=jnp.float32)
        return {'x': x, 'A_shape': A_shape, 'w': w, 'a': a}
    _L0_gnn_all = _L0_gnn_setup()
    _L0_gnn_in = {k: v for k, v in _L0_gnn_all.items() if k in ('w', 'a')}
    del _L0_gnn_all

    def _L1_gnn_setup():
        import jax, jax.numpy as jnp
        import numpy as np
        B, N, DIN, DOUT, K = (4, 1024, 256, 256, 3)
        key = jax.random.key(seed)
        ks = jax.random.split(key, 8)
        X = jax.random.normal(ks[0], (B, N, DIN), dtype=jnp.float32)
        A = jax.random.uniform(ks[1], (B, N, N), dtype=jnp.float32)
        Wv = jax.random.normal(ks[2], (DIN, DOUT), dtype=jnp.float32) * 0.02
        bv = jax.random.normal(ks[3], (DOUT,), dtype=jnp.float32) * 0.02
        aw = jax.random.normal(ks[4], (2 * DOUT, 1), dtype=jnp.float32) * 0.05
        ab = jax.random.normal(ks[5], (1,), dtype=jnp.float32) * 0.05
        Wk = jax.random.normal(ks[6], (K, DIN, DOUT), dtype=jnp.float32) * 0.02
        bk = jax.random.normal(ks[7], (K, DOUT), dtype=jnp.float32) * 0.02
        return {'X': X, 'A': A, 'Wv': Wv, 'bv': bv, 'aw': aw, 'ab': ab, 'Wk': Wk, 'bk': bk}
    _L1_gnn_all = _L1_gnn_setup()
    _L1_gnn_in = {k: v for k, v in _L1_gnn_all.items() if k in ('Wv', 'bv', 'aw', 'ab', 'Wk', 'bk')}
    del _L1_gnn_all
    return {'x': x, 'adj': adj, 'L0_gnn_w': _L0_gnn_in['w'], 'L0_gnn_a': _L0_gnn_in['a'], 'L1_gnn_Wv': _L1_gnn_in['Wv'], 'L1_gnn_bv': _L1_gnn_in['bv'], 'L1_gnn_aw': _L1_gnn_in['aw'], 'L1_gnn_ab': _L1_gnn_in['ab'], 'L1_gnn_Wk': _L1_gnn_in['Wk'], 'L1_gnn_bk': _L1_gnn_in['bk']}

def reference(x, adj, L0_gnn_w, L0_gnn_a, L1_gnn_Wv, L1_gnn_bv, L1_gnn_aw, L1_gnn_ab, L1_gnn_Wk, L1_gnn_bk):
    import jax
    import jax.numpy as jnp

    def _L0_gnn_ref(x, A_shape, w, a):
        import jax, jax.numpy as jnp
        import numpy as np
        B, N, D_IN, D_OUT = (4, 2048, 256, 256)
        y = x @ w
        s = y @ a
        A = s[..., :, None] + s[..., None, :]
        A = jnp.tanh(A / 8.0) * 8.0
        A = jnp.where(A >= 0, A, 0.1 * A)
        A = jnp.exp(A) * A_shape
        A = A / jnp.sum(A, axis=-1, keepdims=True)
        A = A * jnp.sum(A_shape, axis=-1, keepdims=True)
        out = A @ x @ w
        return out

    def _L1_gnn_ref(X, A, Wv, bv, aw, ab, Wk, bk):
        import jax, jax.numpy as jnp
        import numpy as np
        B, N, DIN, DOUT, K = (4, 1024, 256, 256, 3)
        d = Wv.shape[1]
        Xw = X @ Wv + bv
        sj = Xw @ aw[:d, 0]
        si = Xw @ aw[d:, 0]
        e = jax.nn.leaky_relu(sj[:, None, :] + si[:, :, None] + ab[0], negative_slope=0.2)
        alpha_matrix = A * jnp.exp(e)
        transition = alpha_matrix / (jnp.sum(alpha_matrix, axis=-1, keepdims=True) + 1e-12)
        H = jnp.zeros(X.shape[:-1] + (d,), dtype=X.dtype)
        Xk = X
        for k in range(Wk.shape[0]):
            H = H + Xk @ Wk[k] + bk[k]
            Xk = jnp.einsum('bij,bjd->bid', transition, Xk)
        return jax.nn.relu(H)
    x = _layernorm(x + _L0_gnn_ref(x, adj, L0_gnn_w, L0_gnn_a), axis=-1)
    x = _layernorm(x + _L1_gnn_ref(x, adj, L1_gnn_Wv, L1_gnn_bv, L1_gnn_aw, L1_gnn_ab, L1_gnn_Wk, L1_gnn_bk), axis=-1)
    return x

_drawn_inputs = setup_inputs


def setup_inputs(seed=0):
    import zlib

    import numpy as np

    out = dict(_drawn_inputs(seed))
    spreads = {}
    factors = {'L1_gnn_Wv': 4.674, 'L1_gnn_bv': 30.698, 'L1_gnn_aw': 4.417}
    for name, (base, spread) in spreads.items():
        noise = np.random.default_rng([zlib.crc32(name.encode()), seed]).standard_normal(out[name].shape)
        drawn = base * np.exp(spread * noise) if base else spread * noise
        out[name] = jnp.asarray(drawn.astype(out[name].dtype))
    for name, factor in factors.items():
        out[name] = (out[name] * factor).astype(out[name].dtype)
    return out
```

```python
from contextlib import ExitStack

import numpy as np

import concourse.bass as bass
from concourse import mybir

F32 = mybir.dt.float32
F16 = mybir.dt.float16
U32 = mybir.dt.uint32
ALU = mybir.AluOpType
ACT = mybir.ActivationFunctionType
AX = mybir.AxisListType

P = 128
SLOTS = 4
EPS = 1e-5
X_SCALE = 2048.0
W_TOP = 2.0 ** 14
EXPONENT = 0x7F800000


def graph_layers_kernel(nc, x, xT, adjT, w, a, Wv, bv, aw, ab, Wk, bk, out):
    B, N, D = x.shape
    K = Wk.shape[0]
    T = N // P
    C = D // P
    assert N == D == 2 * P and K == 3 and B % SLOTS == 0
    BLOCKS = B // SLOTS

    s0_row = nc.dram_tensor("s0_row", [B, N], F32, kind="Internal").ap()
    s1_row = nc.dram_tensor("s1_row", [B, N], F32, kind="Internal").ap()

    with ExitStack() as ctx:
        def sb(name, shape, dt=F32):
            return ctx.enter_context(nc.sbuf_tensor(name, shape, dt))

        def ps(name, shape, dt=F32):
            return ctx.enter_context(nc.psum_tensor(name, shape, dt))

        def sem(name):
            return ctx.enter_context(nc.semaphore(name))

        def sems(name):
            return [sem(f"{name}{i}") for i in range(SLOTS)]

        w_a = sb("w_a", [P, C, D + 1])
        a_all = sb("a_all", [P, D])
        wv = sb("wv", [P, C, D])
        aw_all = sb("aw_all", [P, 2, D])
        bv_all = sb("bv_all", [P, D])
        ab_all = sb("ab_all", [P, 1])
        bk_all = sb("bk_all", [P, K, D])
        b_sum = sb("b_sum", [P, D])
        W = sb("W", [P, K, C, D])
        v = sb("v", [P, C, 2])
        Wh = sb("Wh", [P, C, K * D + 2], F16)
        Wl = sb("Wl", [P, C, K * D + 2], F16)
        product = sb("product", [P, 4 * C, D])
        top = sb("top", [P, K + 1])
        top_all = sb("top_all", [P, K + 1])
        power = sb("power", [P, K + 1])
        up = sb("up", [P, K + 1])
        down = sb("down", [P, K + 1])
        c_bias = sb("c_bias", [P, 3])
        s1_bias = sb("s1_bias", [P, 1])
        identity32 = sb("identity32", [P, P])
        identity = sb("identity", [P, P], F16)
        ones = sb("ones", [P, 1])
        minus_half = sb("minus_half", [P, T])
        eps = sb("eps", [P, T])

        xT_in = sb("xT_in", [P, SLOTS, C, N])
        x_in = sb("x_in", [P, SLOTS, T, D])
        adj_in = sb("adj_in", [P, SLOTS, T, N])
        y = sb("y", [P, SLOTS, T, D + 1])
        s0 = sb("s0", [P, SLOTS, T])
        s0_all = sb("s0_all", [P, SLOTS, N])
        E0 = sb("E0", [P, SLOTS, T, N])
        adj_half = sb("adj_half", [P, SLOTS, N])
        inv0 = sb("inv0", [P, SLOTS, T])
        r0 = sb("r0", [P, SLOTS, T])
        X1 = sb("X1", [P, SLOTS, T, D])
        bn0 = sb("bn0", [P, SLOTS, T, 6])
        mv0 = sb("mv0", [P, SLOTS, T, 2])
        var0 = sb("var0", [P, SLOTS, T])
        rstd0 = sb("rstd0", [P, SLOTS, T])
        waiter0 = sb("waiter0", [P, SLOTS, 1])
        waiter1 = sb("waiter1", [P, SLOTS, 1])
        Xhl = sb("Xhl", [P, 2, 2, T, D], F16)
        XT = sb("XT", [P, 2, 2, C, T, P], F16)
        G = sb("G", [P, SLOTS, T, D + 1])
        V1 = sb("V1", [P, SLOTS, T, D])
        V0 = sb("V0", [P, SLOTS, T, D])
        s1i = sb("s1i", [P, SLOTS, T])
        s1j = sb("s1j", [P, SLOTS, T])
        s1_all = sb("s1_all", [P, SLOTS, N])
        E1 = sb("E1", [P, SLOTS, T, N])
        den1 = sb("den1", [P, SLOTS, T])
        r1 = sb("r1", [P, SLOTS, T])
        U = sb("U", [P, SLOTS, T, D])
        H = sb("H", [P, SLOTS, T, D])
        bn1 = sb("bn1", [P, SLOTS, T, 6])
        mv1 = sb("mv1", [P, SLOTS, T, 2])
        var1 = sb("var1", [P, SLOTS, T])
        rstd1 = sb("rstd1", [P, SLOTS, T])
        shift1 = sb("shift1", [P, SLOTS, T])
        res = sb("res", [P, SLOTS, T, D])

        pY = ps("pY", [P, T, 512])
        pX = ps("pX", [P, T, 512])
        p1 = ps("p1", [P, T, D])
        p0 = ps("p0", [P, T, D])
        pU = ps("pU", [P, T, D])
        pT = ps("pT", [P, 2, C, T, P], F16)

        ld_w, ld_a, ld_const, ld_W = sem("ld_w"), sem("ld_a"), sem("ld_const"), sem("ld_W")
        const_step = sem("const_step")
        id_step, top_reduced = sem("id_step"), sem("top_reduced")
        wa_ready, W_ready = sem("wa_ready"), sem("W_ready")
        xT_landed, x_landed, adj_landed = sems("xT_landed"), sems("x_landed"), sems("adj_landed")
        s0_sent, s1_sent = sem("s0_sent"), sem("s1_sent")
        s0_landed, s1_landed, stored = sems("s0_landed"), sems("s1_landed"), sems("stored")
        embedded, y_kept, s0_ready = sem("embedded"), sem("y_kept"), sem("s0_ready")
        tanh0, lrelu0, exp0, E0_ready, adj_summed = (
            sem("tanh0"), sem("lrelu0"), sem("exp0"), sem("E0_ready"), sem("adj_summed"))
        attended0, inv0_ready, r0_ready, h_ready = (
            sem("attended0"), sem("inv0_ready"), sem("r0_ready"), sem("h_ready"))
        bn0_ready, mv0_ready, var0_ready, rstd0_ready, X1_ready = (
            sem("bn0_ready"), sem("mv0_ready"), sem("var0_ready"), sem("rstd0_ready"), sem("X1_ready"))
        high_ready, low_ready, turned, XT_kept = (
            sem("high_ready"), sem("low_ready"), sem("turned"), sem("XT_kept"))
        weighed2, weighed1, weighed0 = sem("weighed2"), sem("weighed1"), sem("weighed0")
        G_kept, V1_kept, V0_kept, s1_ready = sem("G_kept"), sem("V1_kept"), sem("V0_kept"), sem("s1_ready")
        z1, lrelu1, exp1, E1_ready = sem("z1"), sem("lrelu1"), sem("exp1"), sem("E1_ready")
        hopped1, den1_ready, r1_ready, U_ready = (
            sem("hopped1"), sem("den1_ready"), sem("r1_ready"), sem("U_ready"))
        hopped2, H_ready, relu_added = sem("hopped2"), sem("H_ready"), sem("relu_added")
        bn1_ready, mv1_ready, var1_ready, rstd1_ready, res_ready = (
            sem("bn1_ready"), sem("mv1_ready"), sem("var1_ready"), sem("rstd1_ready"), sem("res_ready"))

        shift_ready = sem("shift_ready")

        block = ctx.enter_context(nc.Block())

        class Graph:

            def __init__(self, q, u, back):
                self.q, self.slot = q + (u - back) // SLOTS, (u - back) % SLOTS
                self.half = self.slot % 2
                self.number = self.q * SLOTS + self.slot
                self.exists = not isinstance(q, int) or 0 <= self.number < B

        def done(eng, sem_, g, ahead=0):
            n = g.number + ahead + 1
            if isinstance(n, int):
                n = min(n, B)
                if n <= 0:
                    return
            eng.wait_ge(sem_, n)

        def landed(eng, slot_sems, g, ago=0):
            n = 16 * (g.q + 1 - ago)
            if isinstance(n, int) and n <= 0:
                return
            eng.wait_ge(slot_sems[g.slot], n)

        def pipeline(eng, one_round):
            for u in range(SLOTS):
                one_round(0, u)
            with eng.Fori(1, BLOCKS) as q:
                for u in range(SLOTS):
                    one_round(q, u)
            for u in range(SLOTS):
                one_round(BLOCKS, u)

        def load(sp, g):
            done(sp, embedded, g, -SLOTS)
            sp.dma_start(xT_in[:, g.slot], xT[g.number].rearrange("(p c) n -> p c n", c=C))\
                .then_inc(xT_landed[g.slot], 16)
            done(sp, h_ready, g, -SLOTS)
            sp.dma_start(x_in[:, g.slot], x[g.number].rearrange("(p t) d -> p t d", t=T))\
                .then_inc(x_landed[g.slot], 16)

        def load_adj(sp, g):
            done(sp, E1_ready, g, -SLOTS)
            sp.dma_start(adj_in[:, g.slot], adjT[g.number].rearrange("(p t) n -> p t n", t=T))\
                .then_inc(adj_landed[g.slot], 16)

        @block.sync
        def _(sp):
            sp.dma_start(w_a[:, :, 0:D], w.rearrange("(p c) o -> p c o", c=C)).then_inc(ld_w, 16)
            sp.dma_start(a_all[:, :], a[None, :].to_broadcast([P, D])).then_inc(ld_a, 16)
            sp.dma_start(wv[:, :, :], Wv.rearrange("(c p) o -> p c o", p=P)).then_inc(ld_const, 16)
            sp.dma_start(aw_all[:, :, :], aw.rearrange("(s d) o -> o s d", s=2).to_broadcast([P, 2, D]))\
                .then_inc(ld_const, 16)
            sp.dma_start(bv_all[:, :], bv[None, :].to_broadcast([P, D])).then_inc(ld_const, 16)
            sp.dma_start(ab_all[:, :], ab[None, :].to_broadcast([P, 1])).then_inc(ld_const, 16)
            sp.dma_start(bk_all[:, :, :], bk[None, :, :].to_broadcast([P, K, D])).then_inc(ld_const, 16)
            for k in range(K):
                sp.dma_start(W[:, k], Wk[k].rearrange("(c p) o -> p c o", p=P)).then_inc(ld_W, 16)

            def one_round(q, u):
                g0, g1 = Graph(q, u, 1), Graph(q, u, 3)
                if g0.exists:
                    done(sp, s0_ready, g0)
                    sp.dma_start(s0_row[g0.number].rearrange("(p t) -> p t", t=T), s0[:, g0.slot])\
                        .then_inc(s0_sent, 16)
                g = Graph(q, u, 0)
                if g.exists:
                    load(sp, g)
                if g0.exists:
                    sp.wait_ge(s0_sent, (g0.number + 1) * 16)
                    sp.dma_start(s0_all[:, g0.slot], s0_row[g0.number][None, :].to_broadcast([P, N]))\
                        .then_inc(s0_landed[g0.slot], 16)
                if g1.exists:
                    done(sp, s1_ready, g1)
                    sp.dma_start(s1_row[g1.number].rearrange("(p t) -> p t", t=T), s1i[:, g1.slot])\
                        .then_inc(s1_sent, 16)
                if g.exists:
                    load_adj(sp, g)
                if g1.exists:
                    sp.wait_ge(s1_sent, (g1.number + 1) * 16)
                    sp.dma_start(s1_all[:, g1.slot], s1_row[g1.number][None, :].to_broadcast([P, N]))\
                        .then_inc(s1_landed[g1.slot], 16)

            pipeline(sp, one_round)

        @block.tensor
        def _(pe):
            def embed(g):
                landed(pe, xT_landed, g)
                done(pe, y_kept, g, -1)
                done(pe, h_ready, g, -2)
                for t in range(T):
                    for c in range(C):
                        last = nc.tensor.matmul(pY[:, t, 0:D + 1], xT_in[:, g.slot, c, t:N:T], w_a[:, c, :],
                                                start=(c == 0), stop=(c == C - 1))
                last.then_inc(embedded, 1)

            def attend0(g):
                done(pe, E0_ready, g)
                done(pe, adj_summed, g)
                done(pe, y_kept, g, 1)
                done(pe, h_ready, g, -1)
                for t in range(T):
                    for j in range(T):
                        nc.tensor.matmul(pY[:, t, 0:D + 1], E0[:, g.slot, j, t:N:T], y[:, g.slot, j, :],
                                         start=(j == 0), stop=(j == T - 1))
                    last = nc.tensor.matmul(pY[:, t, D + 1:D + 2], adj_half[:, g.slot, t:N:T], ones[:, :],
                                            start=True, stop=True)
                last.then_inc(attended0, 1)

            def turn(g):
                done(pe, high_ready, g)
                done(pe, low_ready, g)
                done(pe, XT_kept, g, -1)
                for part in range(2):
                    for c in range(C):
                        for t in range(T):
                            last = nc.tensor.transpose(pT[:, part, c, t, :],
                                                       Xhl[:, g.half, part, t, c * P:(c + 1) * P], identity[:, :])
                last.then_inc(turned, 1)

            def weigh(g, bank, lo, hi, signal):
                for t in range(T):
                    n = 0
                    for c in range(C):
                        for xp, wp in ((0, Wh), (0, Wl), (1, Wh)):
                            last = nc.tensor.matmul(bank[:, t, 0:hi - lo], XT[:, g.half, xp, c, t, :],
                                                    wp[:, c, lo:hi], start=(n == 0), stop=(n == 3 * C - 1))
                            n += 1
                last.then_inc(signal, 1)

            def weights2(g):
                done(pe, XT_kept, g)
                done(pe, G_kept, g, -1)
                done(pe, U_ready, g, -2)
                weigh(g, pX, 0, D + 2, weighed2)

            def weights1(g):
                done(pe, V1_kept, g, -1)
                weigh(g, p1, D + 2, 2 * D + 2, weighed1)

            def weights0(g):
                done(pe, V0_kept, g, -1)
                weigh(g, p0, 2 * D + 2, 3 * D + 2, weighed0)

            def hop1(g):
                done(pe, E1_ready, g)
                done(pe, G_kept, g, 1)
                done(pe, U_ready, g, -1)
                for t in range(T):
                    for j in range(T):
                        last = nc.tensor.matmul(pX[:, t, 0:D + 1], E1[:, g.slot, j, t:N:T], G[:, g.slot, j, :],
                                                start=(j == 0), stop=(j == T - 1))
                last.then_inc(hopped1, 1)

            def hop2(g):
                done(pe, U_ready, g)
                done(pe, H_ready, g, -1)
                for t in range(T):
                    for j in range(T):
                        last = nc.tensor.matmul(pU[:, t, :], E1[:, g.slot, j, t:N:T], U[:, g.slot, j, :],
                                                start=(j == 0), stop=(j == T - 1))
                last.then_inc(hopped2, 1)

            pe.wait_ge(wa_ready, 3)

            def one_round(q, u):
                for back, step in ((2, attend0), (4, hop1), (3, weights0), (3, weights1), (4, hop2), (2, turn),
                                   (0, embed), (2, weights2)):
                    g = Graph(q, u, back)
                    if g.exists:
                        if step is turn and isinstance(q, int) and q == 0 and g.number == 0:
                            pe.wait_ge(W_ready, 1)
                        step(g)

            pipeline(pe, one_round)

        @block.scalar
        def _(act):
            def keep_V1(g):
                done(act, weighed1, g)
                nc.scalar.activation(V1[:, g.slot], p1[:, :, :], ACT.Copy, scale=down[:, 1:2]).then_inc(V1_kept, 1)

            def tanh(g):
                landed(act, s0_landed, g)
                for j in range(T):
                    last = nc.scalar.activation(E0[:, g.slot, j, :], s0_all[:, g.slot, :], ACT.Tanh,
                                                bias=s0[:, g.slot, j:j + 1])
                last.then_inc(tanh0, 1)

            def exp_0(g):
                done(act, lrelu0, g)
                nc.scalar.activation(E0[:, g.slot], E0[:, g.slot], ACT.Exp, scale=8.0).then_inc(exp0, 1)

            def z(g):
                landed(act, s1_landed, g)
                for j in range(T):
                    last = nc.scalar.activation(E1[:, g.slot, j, :], s1_all[:, g.slot, :], ACT.Identity,
                                                bias=s1j[:, g.slot, j:j + 1])
                last.then_inc(z1, 1)

            def exp_1(g):
                done(act, lrelu1, g)
                nc.scalar.activation(E1[:, g.slot], E1[:, g.slot], ACT.Exp).then_inc(exp1, 1)

            def high(g):
                done(act, X1_ready, g)
                nc.scalar.activation(Xhl[:, g.half, 0], X1[:, g.slot], ACT.Copy, scale=X_SCALE).then_inc(high_ready, 1)

            def keep_XT(g):
                done(act, turned, g)
                nc.scalar.activation(XT[:, g.half], pT[:, :, :, :, :], ACT.Copy).then_inc(XT_kept, 1)

            def keep_y(g):
                done(act, s0_ready, g)
                nc.scalar.activation(y[:, g.slot, :, 0:D], pY[:, :, 0:D], ACT.Copy).then_inc(y_kept, 1)

            def keep_G(g):
                done(act, s1_ready, g)
                nc.scalar.activation(G[:, g.slot, :, 0:D], pX[:, :, 0:D], ACT.Copy, scale=down[:, 2:3])\
                    .then_inc(G_kept, 1)

            def finish(g):
                done(act, shift_ready, g)
                landed(act, stored, g, 1)
                for t in range(T):
                    last = nc.scalar.activation(res[:, g.slot, t, :], H[:, g.slot, t, :], ACT.Identity,
                                                bias=shift1[:, g.slot, t:t + 1], scale=rstd1[:, g.slot, t:t + 1])
                last.then_inc(res_ready, 1)
                done(act, res_ready, g)
                act.dma_start(out[g.number].rearrange("(p t) d -> p t d", t=T), res[:, g.slot])\
                    .then_inc(stored[g.slot], 16)

            def one_round(q, u):
                for back, step in ((1, tanh), (2, high), (3, z), (1, exp_0), (3, keep_V1), (3, exp_1), (2, keep_XT),
                                   (0, keep_y), (2, keep_G), (4, finish)):
                    g = Graph(q, u, back)
                    if g.exists:
                        step(g)

            pipeline(act, one_round)
            for slot in range(SLOTS):
                act.wait_ge(stored[slot], 16 * BLOCKS)

        @block.gpsimd
        def _(pool):
            nc.gpsimd.memset(identity32[:, :], 0.0).then_inc(id_step, 1)
            nc.gpsimd.memset(ones[:, :], 1.0).then_inc(wa_ready, 1)
            nc.gpsimd.memset(minus_half[:, :], -0.5).then_inc(id_step, 1)
            nc.gpsimd.memset(eps[:, :], EPS).then_inc(id_step, 1)
            nc.gpsimd.memset(y[:, :, :, D:D + 1], 1.0).then_inc(wa_ready, 1)
            nc.gpsimd.memset(G[:, :, :, D:D + 1], 1.0).then_inc(id_step, 1)
            pool.wait_ge(id_step, 4)
            nc.gpsimd.affine_select(out=identity32[:, :], in_=identity32[:, :], compare_op=ALU.not_equal, fill=1.0,
                                    base=0, pattern=[[-1, P]], channel_multiplier=1).then_inc(id_step, 1)
            pool.wait_ge(const_step, 2)
            nc.gpsimd.partition_all_reduce(top_all[:, :], top[:, :], P, bass.bass_isa.ReduceOp.max)\
                .then_inc(top_reduced, 1)

            def sum_adj(g):
                landed(pool, adj_landed, g)
                done(pool, attended0, g, -SLOTS)
                nc.gpsimd.tensor_tensor(adj_half[:, g.slot], adj_in[:, g.slot, 0, :], adj_in[:, g.slot, 1, :], ALU.add)\
                    .then_inc(adj_summed, 1)

            def inverse_std(g, mv, mv_ready, var, var_ready, rstd, rstd_ready):
                done(pool, mv_ready, g)
                nc.gpsimd.tensor_tensor(var[:, g.slot], mv[:, g.slot, :, 1], eps[:, :], ALU.add).then_inc(var_ready, 1)
                done(pool, var_ready, g)
                nc.gpsimd.tensor_tensor(rstd[:, g.slot], var[:, g.slot], minus_half[:, :], ALU.pow)\
                    .then_inc(rstd_ready, 1)

            def std0(g):
                inverse_std(g, mv0, mv0_ready, var0, var0_ready, rstd0, rstd0_ready)

            def times_adj0(g):
                done(pool, exp0, g)
                nc.gpsimd.tensor_tensor(E0[:, g.slot], E0[:, g.slot], adj_in[:, g.slot], ALU.mult).then_inc(E0_ready, 1)

            def times_adj1(g):
                done(pool, exp1, g)
                nc.gpsimd.tensor_tensor(E1[:, g.slot], E1[:, g.slot], adj_in[:, g.slot], ALU.mult).then_inc(E1_ready, 1)

            def std1(g):
                inverse_std(g, mv1, mv1_ready, var1, var1_ready, rstd1, rstd1_ready)

            def one_round(q, u):
                for back, step in ((1, sum_adj), (2, std0), (1, times_adj0), (3, times_adj1), (4, std1)):
                    g = Graph(q, u, back)
                    if g.exists:
                        step(g)

            pipeline(pool, one_round)

        @block.vector
        def _(dve):
            dve.wait_ge(ld_w, 16)
            dve.wait_ge(ld_a, 16)
            for c in range(C):
                last = nc.vector.tensor_tensor_reduce(product[:, c, :], w_a[:, c, 0:D], a_all[:, :], 1.0, 0.0, ALU.mult,
                                                      ALU.add, w_a[:, c, D:D + 1])
            last.then_inc(wa_ready, 1)

            def constants():
                steps = [0]

                def chained(instruction):
                    steps[0] += 1
                    instruction.then_inc(const_step, 1)
                    dve.wait_ge(const_step, steps[0])

                dve.wait_ge(ld_const, 16 * 5)
                for i in range(2):
                    for c in range(C):
                        nc.vector.tensor_tensor_reduce(product[:, C * (i + 1) + c, :], wv[:, c, :], aw_all[:, i, :], 1.0, 0.0, ALU.mult,
                                                       ALU.add, v[:, c, i:i + 1])
                    last = nc.vector.tensor_tensor_reduce(product[:, 3 * C + i, :], bv_all[:, :], aw_all[:, i, :], 1.0,
                                                          0.0, ALU.mult, ALU.add, c_bias[:, i:i + 1])
                chained(last)
                dve.wait_ge(ld_W, 16 * K)
                for k in range(K):
                    nc.vector.tensor_reduce(top[:, k:k + 1], W[:, k], AX.XY, ALU.max, apply_absolute_value=True)
                chained(nc.vector.tensor_reduce(top[:, K:K + 1], v[:, :, :], AX.XY, ALU.max, apply_absolute_value=True))
                chained(nc.vector.tensor_tensor(c_bias[:, 2:3], c_bias[:, 0:1], c_bias[:, 1:2], ALU.add))
                chained(nc.vector.tensor_tensor(s1_bias[:, :], c_bias[:, 2:3], ab_all[:, :], ALU.add))
                chained(nc.vector.tensor_tensor(b_sum[:, :], bk_all[:, 0, :], bk_all[:, 1, :], ALU.add))
                chained(nc.vector.tensor_tensor(b_sum[:, :], b_sum[:, :], bk_all[:, 2, :], ALU.add))
                dve.wait_ge(top_reduced, 1)
                chained(nc.vector.tensor_scalar(top[:, :], top_all[:, :], 1e-30, None, ALU.max))
                chained(nc.vector.tensor_scalar(power[:, :].bitcast(U32), top[:, :].bitcast(U32), EXPONENT, None,
                                                ALU.bitwise_and))
                chained(nc.vector.reciprocal(up[:, :], power[:, :]))
                chained(nc.vector.tensor_scalar(up[:, :], up[:, :], W_TOP, None, ALU.mult))
                chained(nc.vector.tensor_scalar(down[:, :], power[:, :], 1.0 / (W_TOP * X_SCALE), None, ALU.mult))
                parts = ((W[:, 2], 2, 0, D), (v[:, :, :], 3, D, D + 2), (W[:, 1], 1, D + 2, 2 * D + 2),
                         (W[:, 0], 0, 2 * D + 2, 3 * D + 2))
                for src, k, lo, hi in parts:
                    chained(nc.vector.tensor_scalar(Wh[:, :, lo:hi], src, up[:, k:k + 1], None, ALU.mult))
                for src, k, lo, hi in parts:
                    chained(nc.vector.scalar_tensor_tensor(out=Wl[:, :, lo:hi], in0=src, scalar=up[:, k:k + 1],
                                                           in1=Wh[:, :, lo:hi], op0=ALU.mult, op1=ALU.subtract))
                dve.wait_ge(id_step, 5)
                nc.vector.tensor_copy(identity[:, :], identity32[:, :]).then_inc(W_ready, 1)

            def residual0(g):
                done(dve, attended0, g)
                nc.vector.reciprocal(inv0[:, g.slot], pY[:, :, D]).then_inc(inv0_ready, 1)
                done(dve, inv0_ready, g)
                nc.vector.tensor_tensor(r0[:, g.slot], pY[:, :, D + 1], inv0[:, g.slot], ALU.mult).then_inc(r0_ready, 1)
                done(dve, r0_ready, g)
                landed(dve, x_landed, g)
                for t in range(T):
                    last = nc.vector.scalar_tensor_tensor(out=X1[:, g.slot, t, :], in0=pY[:, t, 0:D],
                                                          scalar=r0[:, g.slot, t:t + 1], in1=x_in[:, g.slot, t, :],
                                                          op0=ALU.mult, op1=ALU.add)
                last.then_inc(h_ready, 1)
                done(dve, h_ready, g)
                moments(g, X1, bn0, bn0_ready, mv0, mv0_ready, waiter0)

            def moments(g, rows, bn, bn_ready, mv, mv_ready, waiter):
                for t in range(T):
                    last = nc.vector.bn_stats(bn[:, g.slot, t, :], rows[:, g.slot, t, :])
                last.then_inc(bn_ready, 1)
                done(dve, bn_ready, g)
                nc.vector.memset(waiter[:, g.slot], 0.0)
                for t in range(T):
                    last = nc.vector.bn_aggr(mv[:, g.slot, t, :], bn[:, g.slot, t, :])
                last.then_inc(mv_ready, 1)

            def add_V1(g):
                done(dve, hopped1, g)
                nc.vector.tensor_scalar(den1[:, g.slot], pX[:, :, D], 1e-12, None, ALU.add).then_inc(den1_ready, 1)
                done(dve, den1_ready, g)
                nc.vector.reciprocal(r1[:, g.slot], den1[:, g.slot]).then_inc(r1_ready, 1)
                done(dve, r1_ready, g)
                done(dve, V1_kept, g)
                for t in range(T):
                    last = nc.vector.scalar_tensor_tensor(out=U[:, g.slot, t, :], in0=pX[:, t, 0:D],
                                                          scalar=r1[:, g.slot, t:t + 1], in1=V1[:, g.slot, t, :],
                                                          op0=ALU.mult, op1=ALU.add)
                last.then_inc(U_ready, 1)

            def norm0(g):
                done(dve, rstd0_ready, g)
                for t in range(T):
                    last = nc.vector.tensor_scalar(X1[:, g.slot, t, :], X1[:, g.slot, t, :], mv0[:, g.slot, t, 0:1],
                                                   rstd0[:, g.slot, t:t + 1], ALU.subtract, ALU.mult)
                last.then_inc(X1_ready, 1)

            def leaky0(g):
                done(dve, tanh0, g)
                nc.vector.scalar_tensor_tensor(out=E0[:, g.slot], in0=E0[:, g.slot], scalar=0.1, in1=E0[:, g.slot],
                                               op0=ALU.mult, op1=ALU.max).then_inc(lrelu0, 1)

            def leaky1(g):
                done(dve, z1, g)
                nc.vector.scalar_tensor_tensor(out=E1[:, g.slot], in0=E1[:, g.slot], scalar=0.2, in1=E1[:, g.slot],
                                               op0=ALU.mult, op1=ALU.max).then_inc(lrelu1, 1)

            def low(g):
                done(dve, high_ready, g)
                nc.vector.scalar_tensor_tensor(out=Xhl[:, g.half, 1], in0=X1[:, g.slot], scalar=X_SCALE,
                                               in1=Xhl[:, g.half, 0], op0=ALU.mult, op1=ALU.subtract)\
                    .then_inc(low_ready, 1)

            def keep_V0(g):
                done(dve, weighed0, g)
                nc.vector.scalar_tensor_tensor(out=V0[:, g.slot], in0=p0[:, :, :], scalar=down[:, 0:1],
                                               in1=b_sum[:, None, :].to_broadcast([P, T, D]),
                                               op0=ALU.mult, op1=ALU.add).then_inc(V0_kept, 1)

            def residual1(g):
                done(dve, hopped2, g)
                done(dve, V0_kept, g)
                for t in range(T):
                    last = nc.vector.scalar_tensor_tensor(out=H[:, g.slot, t, :], in0=pU[:, t, :],
                                                          scalar=r1[:, g.slot, t:t + 1], in1=V0[:, g.slot, t, :],
                                                          op0=ALU.mult, op1=ALU.add)
                last.then_inc(H_ready, 1)

            def relu_add(g):
                done(dve, H_ready, g)
                nc.vector.scalar_tensor_tensor(out=H[:, g.slot], in0=H[:, g.slot], scalar=0.0, in1=X1[:, g.slot],
                                               op0=ALU.max, op1=ALU.add).then_inc(relu_added, 1)
                done(dve, relu_added, g)
                moments(g, H, bn1, bn1_ready, mv1, mv1_ready, waiter1)

            def shift(g):
                done(dve, rstd1_ready, g)
                nc.vector.scalar_tensor_tensor(out=shift1[:, g.slot], in0=mv1[:, g.slot, :, 0], scalar=-1.0,
                                               in1=rstd1[:, g.slot], op0=ALU.mult, op1=ALU.mult).then_inc(shift_ready, 1)

            def s0_column(g):
                done(dve, embedded, g)
                nc.vector.tensor_scalar(s0[:, g.slot], pY[:, :, D], 0.125, None, ALU.mult).then_inc(s0_ready, 1)

            def s1_columns(g):
                done(dve, weighed2, g)
                nc.vector.tensor_scalar(s1j[:, g.slot], pX[:, :, D], down[:, 3:4], None, ALU.mult)
                nc.vector.tensor_scalar(s1i[:, g.slot], pX[:, :, D + 1], down[:, 3:4], s1_bias[:, 0:1],
                                        ALU.mult, ALU.add).then_inc(s1_ready, 1)

            def one_round(q, u):
                for back, step in ((2, residual0), (4, add_V1), (2, norm0), (1, leaky0), (2, low), (3, leaky1),
                                   (3, keep_V0), (4, residual1), (0, s0_column), (4, relu_add), (2, s1_columns), (4, shift)):
                    g = Graph(q, u, back)
                    if g.exists:
                        step(g)
                if isinstance(q, int) and q == 0 and u == 0:
                    constants()

            pipeline(dve, one_round)


_ORDER = ["x", "xT", "adjT", "w", "a", "Wv", "bv", "aw", "ab", "Wk", "bk"]


def kernel(x, adj, L0_gnn_w, L0_gnn_a, L1_gnn_Wv, L1_gnn_bv, L1_gnn_aw, L1_gnn_ab, L1_gnn_Wk, L1_gnn_bk):
    import concourse.bacc as bacc
    from concourse.bass_utils import run_bass_kernel_spmd

    x, adj = np.asarray(x), np.asarray(adj)
    inputs = {
        "x": x, "xT": x.transpose(0, 2, 1), "adjT": adj.transpose(0, 2, 1), "w": L0_gnn_w, "a": L0_gnn_a,
        "Wv": L1_gnn_Wv, "bv": L1_gnn_bv, "aw": L1_gnn_aw, "ab": L1_gnn_ab, "Wk": L1_gnn_Wk, "bk": L1_gnn_bk,
    }
    nc = bacc.Bacc("TRN2", target_bir_lowering=False, num_devices=1)
    arrays, args = {}, []
    for name in _ORDER:
        array = np.ascontiguousarray(np.asarray(inputs[name]))
        arrays[f"in_{name}"] = array
        args.append(nc.dram_tensor(f"in_{name}", array.shape, mybir.dt.from_np(array.dtype), kind="ExternalInput").ap())
    result = nc.dram_tensor("result", x.shape, F32, kind="ExternalOutput").ap()
    graph_layers_kernel(nc, *args, result)
    run = run_bass_kernel_spmd(nc, [arrays], core_ids=[0])
    return run.results[0]["result"]
```

```python
from contextlib import ExitStack

import numpy as np

import concourse.bass as bass
from concourse import mybir

F32 = mybir.dt.float32
F16 = mybir.dt.float16
U32 = mybir.dt.uint32
ALU = mybir.AluOpType
ACT = mybir.ActivationFunctionType
AX = mybir.AxisListType

P = 128
SLOTS = 4
EPS = 1e-5
X_SCALE = 2048.0
W_TOP = 2.0 ** 14
EXPONENT = 0x7F800000


def graph_layers_kernel(nc, x, xT, adj, adjT, w, a, Wv, bv, aw, ab, Wk, bk, out):
    B, N, D = x.shape
    K = Wk.shape[0]
    T = N // P
    C = D // P
    assert N == D == 2 * P and K == 3 and B % SLOTS == 0
    BLOCKS = B // SLOTS

    s0_row = nc.dram_tensor("s0_row", [B, N], F32, kind="Internal").ap()
    s1_row = nc.dram_tensor("s1_row", [B, N], F32, kind="Internal").ap()

    with ExitStack() as ctx:
        def sb(name, shape, dt=F32):
            return ctx.enter_context(nc.sbuf_tensor(name, shape, dt))

        def ps(name, shape, dt=F32):
            return ctx.enter_context(nc.psum_tensor(name, shape, dt))

        def sem(name):
            return ctx.enter_context(nc.semaphore(name))

        def sems(name):
            return [sem(f"{name}{i}") for i in range(SLOTS)]

        w_a = sb("w_a", [P, C, D + 1])
        a_all = sb("a_all", [P, D])
        wv = sb("wv", [P, C, D])
        aw_all = sb("aw_all", [P, 2, D])
        bv_all = sb("bv_all", [P, D])
        ab_all = sb("ab_all", [P, 1])
        bk_all = sb("bk_all", [P, K, D])
        b_sum = sb("b_sum", [P, D])
        W = sb("W", [P, K, C, D])
        v = sb("v", [P, C, 2])
        Wh = sb("Wh", [P, C, K * D + 2], F16)
        Wl = sb("Wl", [P, C, K * D + 2], F16)
        product = sb("product", [P, 4 * C, D])
        top = sb("top", [P, K + 1])
        top_all = sb("top_all", [P, K + 1])
        power = sb("power", [P, K + 1])
        inv_power = sb("inv_power", [P, K + 1])
        up = sb("up", [P, K + 1])
        down = sb("down", [P, K + 1])
        c_bias = sb("c_bias", [P, 3])
        s1_bias = sb("s1_bias", [P, T, 2])
        identity32 = sb("identity32", [P, P])
        identity = sb("identity", [P, P], F16)
        ones = sb("ones", [P, P])
        minus_half = sb("minus_half", [P, T])
        eps = sb("eps", [P, T])

        weight_parts = ((W[:, 2], 2, 0, D), (v[:, :, :], 3, D, D + 2), (W[:, 1], 1, D + 2, 2 * D + 2),
                        (W[:, 0], 0, 2 * D + 2, 3 * D + 2))

        diagonal = sb("diagonal", [P, 5, T, P])

        xT_in = sb("xT_in", [P, SLOTS, C, N])
        x_in = sb("x_in", [P, SLOTS, T, D])
        adj_in = sb("adj_in", [P, SLOTS, T, N])
        y = sb("y", [P, SLOTS, T, D + 1])
        s0 = sb("s0", [P, SLOTS, T])
        s0_all = sb("s0_all", [P, SLOTS, N])
        E0 = sb("E0", [P, SLOTS, T, N])
        adj_rows = sb("adj_rows", [P, SLOTS, T, N])
        adj_sum = sb("adj_sum", [P, SLOTS, T])
        inv0 = sb("inv0", [P, SLOTS, T])
        r0 = sb("r0", [P, SLOTS, T])
        X1 = sb("X1", [P, SLOTS, T, D])
        bn0 = sb("bn0", [P, SLOTS, T, 6])
        mv0 = sb("mv0", [P, SLOTS, T, 2])
        var0 = sb("var0", [P, SLOTS, T])
        rstd0 = sb("rstd0", [P, SLOTS, T])
        waiter0 = sb("waiter0", [P, SLOTS, 1])
        waiter1 = sb("waiter1", [P, SLOTS, 1])
        Xhl = sb("Xhl", [P, 2, 2, T, D], F16)
        XT = sb("XT", [P, 2, 2, C, T, P], F16)
        G = sb("G", [P, SLOTS, T, D + 1])
        V1 = sb("V1", [P, SLOTS, T, D])
        V0 = sb("V0", [P, SLOTS, T, D])
        s1 = sb("s1", [P, SLOTS, 2, T])
        s1_all = sb("s1_all", [P, SLOTS, N])
        E1 = sb("E1", [P, SLOTS, T, N])
        den1 = sb("den1", [P, SLOTS, T])
        r1 = sb("r1", [P, SLOTS, T])
        U = sb("U", [P, SLOTS, T, D])
        H = sb("H", [P, SLOTS, T, D])
        bn1 = sb("bn1", [P, SLOTS, T, 6])
        mv1 = sb("mv1", [P, SLOTS, T, 2])
        var1 = sb("var1", [P, SLOTS, T])
        rstd1 = sb("rstd1", [P, SLOTS, T])
        shift1 = sb("shift1", [P, SLOTS, T])
        res = sb("res", [P, SLOTS, T, D])

        pY = ps("pY", [P, T, 512])
        pX = ps("pX", [P, T, 512])
        p1 = ps("p1", [P, T, D])
        p0 = ps("p0", [P, T, D])
        pU = ps("pU", [P, T, D])
        pT = ps("pT", [P, 2, C, T, P], F16)

        spread_rows = {("s0", 0): (0, p0[:, 0, :]), ("s0", 1): (1, p1[:, 0, :]), ("s1", 0): (2, pU[:, 0, :]),
                       ("s1", B - 2): (3, pY[:, 1, 0:N]), ("s1", B - 1): (4, pY[:, 0, 0:N])}

        S0_SPREAD, S1_SPREAD = 2, 1

        ld_w, ld_a, ld_const, ld_W = sem("ld_w"), sem("ld_a"), sem("ld_const"), sem("ld_W")
        ld_bk = sem("ld_bk")
        const_step = sem("const_step")
        id_step, identity_ready = sem("id_step"), sem("identity_ready")
        b_sum_step, top_ready, top_reduced = sem("b_sum_step"), sem("top_ready"), sem("top_reduced")
        wa_ready, up_ready, Wh_ready, W_ready = sem("wa_ready"), sem("up_ready"), sem("Wh_ready"), sem("W_ready")
        xT_landed, x_landed = sems("xT_landed"), sems("x_landed")
        adj_landed, rows_landed = sems("adj_landed"), sems("rows_landed")
        s0_sent, s1_sent = sem("s0_sent"), sem("s1_sent")
        s0_landed, s1_landed, stored = sems("s0_landed"), sems("s1_landed"), sems("stored")
        embedded, y_kept, s0_ready = sem("embedded"), sem("y_kept"), sem("s0_ready")
        tanh0, lrelu0, exp0, E0_ready, adj_summed = (
            sem("tanh0"), sem("lrelu0"), sem("exp0"), sem("E0_ready"), sem("adj_summed"))
        attended0, inv0_ready, r0_ready, h_ready = (
            sem("attended0"), sem("inv0_ready"), sem("r0_ready"), sem("h_ready"))
        bn0_ready, mv0_ready, var0_ready, rstd0_ready, X1_ready = (
            sem("bn0_ready"), sem("mv0_ready"), sem("var0_ready"), sem("rstd0_ready"), sem("X1_ready"))
        high_ready, low_ready, turned, XT_kept = (
            sem("high_ready"), sem("low_ready"), sem("turned"), sem("XT_kept"))
        weighed2, weighed1, weighed0 = sem("weighed2"), sem("weighed1"), sem("weighed0")
        G_kept, V1_kept, V0_kept, s1_ready = sem("G_kept"), sem("V1_kept"), sem("V0_kept"), sem("s1_ready")
        z1, lrelu1, exp1, E1_ready = sem("z1"), sem("lrelu1"), sem("exp1"), sem("E1_ready")
        hopped1, den1_ready, r1_ready, U_ready = (
            sem("hopped1"), sem("den1_ready"), sem("r1_ready"), sem("U_ready"))
        hopped2, H_ready, relu_added = sem("hopped2"), sem("H_ready"), sem("relu_added")
        bn1_ready, mv1_ready, var1_ready, rstd1_ready, res_ready = (
            sem("bn1_ready"), sem("mv1_ready"), sem("var1_ready"), sem("rstd1_ready"), sem("res_ready"))

        shift_ready = sem("shift_ready")
        diagonal_ready, row_spread = sem("diagonal_ready"), sem("row_spread")

        block = ctx.enter_context(nc.Block())

        class Graph:

            def __init__(self, q, u, back):
                self.q, self.slot = q + (u - back) // SLOTS, (u - back) % SLOTS
                self.half = self.slot % 2
                self.number = self.q * SLOTS + self.slot

        def done(eng, sem_, g, ahead=0):
            n = g.number + ahead + 1
            if isinstance(n, int):
                n = min(n, B)
                if n <= 0:
                    return
            eng.wait_ge(sem_, n)

        def landed(eng, slot_sems, g, ago=0):
            n = 16 * (g.q + 1 - ago)
            if isinstance(n, int) and n <= 0:
                return
            eng.wait_ge(slot_sems[g.slot], n)

        def steady(eng, steps):
            with eng.Fori(1, BLOCKS) as q:
                for u in range(SLOTS):
                    for step, back in steps:
                        step(Graph(q, u, back))

        def first_bank(g):
            return pX if isinstance(g.q, int) and g.q == 0 and g.number % 2 else pY

        def straight(steps, base=0):
            for step, n in steps:
                if n is None:
                    step()
                else:
                    step(Graph((base + n) // SLOTS, (base + n) % SLOTS, 0))

        @block.sync
        def _(sp):
            sp.dma_start(w_a[:, :, 0:D], w.rearrange("(p c) o -> p c o", c=C)).then_inc(ld_w, 16)
            sp.dma_start(a_all[:, :], a[None, :].to_broadcast([P, D])).then_inc(ld_a, 16)
            def load_xT(g):
                done(sp, embedded, g, -SLOTS)
                sp.dma_start(xT_in[:, g.slot], xT[g.number].rearrange("(p c) n -> p c n", c=C))\
                    .then_inc(xT_landed[g.slot], 16)

            def load_x(g):
                done(sp, h_ready, g, -SLOTS)
                sp.dma_start(x_in[:, g.slot], x[g.number].rearrange("(p t) d -> p t d", t=T))\
                    .then_inc(x_landed[g.slot], 16)

            def load_adj(g):
                done(sp, E1_ready, g, -SLOTS)
                sp.dma_start(adj_in[:, g.slot], adjT[g.number].rearrange("(p t) n -> p t n", t=T))\
                    .then_inc(adj_landed[g.slot], 16)

            def load_rows(g):
                done(sp, adj_summed, g, -SLOTS)
                sp.dma_start(adj_rows[:, g.slot], adj[g.number].rearrange("(p t) n -> p t n", t=T))\
                    .then_inc(rows_landed[g.slot], 16)

            def send_s0(g):
                done(sp, s0_ready, g)
                sp.dma_start(s0_row[g.number].rearrange("(p t) -> p t", t=T), s0[:, g.slot]).then_inc(s0_sent, 16)

            def spread_s0(g):
                sp.wait_ge(s0_sent, (g.number + 1 - S0_SPREAD) * 16)
                sp.dma_start(s0_all[:, g.slot], s0_row[g.number][None, :].to_broadcast([P, N]))\
                    .then_inc(s0_landed[g.slot], 16)

            def send_s1(g):
                done(sp, s1_ready, g)
                sp.dma_start(s1_row[g.number].rearrange("(p t) -> p t", t=T), s1[:, g.slot, 1]).then_inc(s1_sent, 16)

            def spread_s1(g):
                sp.wait_ge(s1_sent, (g.number + 1 - S1_SPREAD) * 16)
                sp.dma_start(s1_all[:, g.slot], s1_row[g.number][None, :].to_broadcast([P, N]))\
                    .then_inc(s1_landed[g.slot], 16)

            straight(((load_xT, 0), (load_xT, 1), (load_xT, 2), (load_adj, 0), (load_xT, 3),
                      (load_rows, 0), (load_x, 0), (load_adj, 1), (load_rows, 1),
                      (send_s0, 2), (load_x, 1), (load_adj, 2), (spread_s0, 2),
                      (load_rows, 2), (load_x, 2), (load_adj, 3), (load_rows, 3), (load_x, 3)))
            steady(sp, ((send_s0, 1), (load_xT, 0), (load_x, 0), (spread_s0, 1), (send_s1, 3), (load_adj, 0),
                        (load_rows, 0), (spread_s1, 3)))
            straight(((send_s0, -1), (spread_s0, -1), (send_s1, -3), (spread_s1, -3)), B)

        @block.tensor
        def _(pe):
            def embed(g, kept=-1, attended=-2):
                landed(pe, xT_landed, g)
                done(pe, y_kept, g, kept)
                done(pe, h_ready, g, attended)
                bank = first_bank(g)
                for t in range(T):
                    for c in range(C):
                        last = nc.tensor.matmul(bank[:, t, 0:D + 1], xT_in[:, g.slot, c, t:N:T], w_a[:, c, :],
                                                start=(c == 0), stop=(c == C - 1))
                last.then_inc(embedded, 1)

            def attend0(g, kept=1, attended=-1):
                done(pe, E0_ready, g)
                done(pe, y_kept, g, kept)
                done(pe, h_ready, g, attended)
                bank = first_bank(g) if attended < -1 else pY
                for t in range(T):
                    for j in range(T):
                        last = nc.tensor.matmul(bank[:, t, 0:D + 1], E0[:, g.slot, j, t:N:T], y[:, g.slot, j, :],
                                                start=(j == 0), stop=(j == T - 1))
                last.then_inc(attended0, 1)

            def turn(g):
                done(pe, high_ready, g)
                done(pe, low_ready, g)
                done(pe, XT_kept, g, -1)
                for part in range(2):
                    for c in range(C):
                        for t in range(T):
                            last = nc.tensor.transpose(pT[:, part, c, t, :],
                                                       Xhl[:, g.half, part, t, c * P:(c + 1) * P], identity[:, :])
                last.then_inc(turned, 1)

            def weigh(g, bank, lo, hi, signal):
                for t in range(T):
                    n = 0
                    for c in range(C):
                        for xp, wp in ((0, Wh), (0, Wl), (1, Wh)):
                            last = nc.tensor.matmul(bank[:, t, 0:hi - lo], XT[:, g.half, xp, c, t, :],
                                                    wp[:, c, lo:hi], start=(n == 0), stop=(n == 3 * C - 1))
                            n += 1
                last.then_inc(signal, 1)

            def weights2(g):
                done(pe, XT_kept, g)
                done(pe, G_kept, g, -1)
                done(pe, U_ready, g, -2)
                weigh(g, pX, 0, D + 2, weighed2)

            def weights1(g):
                done(pe, V1_kept, g, -1)
                weigh(g, p1, D + 2, 2 * D + 2, weighed1)

            def weights0(g):
                done(pe, V0_kept, g, -1)
                weigh(g, p0, 2 * D + 2, 3 * D + 2, weighed0)

            def hop1(g):
                done(pe, E1_ready, g)
                done(pe, G_kept, g, 1)
                done(pe, U_ready, g, -1)
                for t in range(T):
                    for j in range(T):
                        last = nc.tensor.matmul(pX[:, t, 0:D + 1], E1[:, g.slot, j, t:N:T], G[:, g.slot, j, :],
                                                start=(j == 0), stop=(j == T - 1))
                last.then_inc(hopped1, 1)

            def hop2(g):
                done(pe, U_ready, g)
                done(pe, H_ready, g, -1)
                for t in range(T):
                    for j in range(T):
                        last = nc.tensor.matmul(pU[:, t, :], E1[:, g.slot, j, t:N:T], U[:, g.slot, j, :],
                                                start=(j == 0), stop=(j == T - 1))
                last.then_inc(hopped2, 1)

            def embed_first(g):
                embed(g, kept=-2, attended=-SLOTS)

            def attend0_first(g):
                attend0(g, kept=2, attended=-2)

            def spread_row(key):
                n, bank = spread_rows[key]
                pe.wait_ge(diagonal_ready, n + 1)
                for t in range(T):
                    last = nc.tensor.matmul(bank[:, t:N:T], ones[:, :], diagonal[:, n, t, :], start=True, stop=True)
                last.then_inc(row_spread, 1)

            def spread_s0(g):
                spread_row(("s0", g.number))

            def spread_s1(g):
                if g.number == B - 2:
                    pe.wait_ge(h_ready, B)
                spread_row(("s1", g.number))

            def low_W2():
                pe.wait_ge(W_ready, 1)
                pe.wait_ge(h_ready, 2)

            def low_W():
                pe.wait_ge(W_ready, 2)

            pe.wait_ge(wa_ready, 1)
            straight(((embed_first, 0), (embed_first, 1), (spread_s0, 0), (embed_first, 2), (spread_s0, 1),
                      (embed_first, 3),
                      (attend0_first, 0), (attend0_first, 1)))
            pe.wait_ge(identity_ready, 1)
            straight(((turn, 0), (low_W2, None), (weights2, 0), (low_W, None), (weights0, 0), (spread_s1, 0),
                      (turn, 1), (weights1, 0), (weights2, 1)))
            steady(pe, ((attend0, 2), (hop1, 4), (weights0, 3), (weights1, 3), (hop2, 4), (turn, 2), (embed, 0),
                        (weights2, 2)))
            straight(((attend0, -2), (hop1, -4), (weights0, -3), (weights1, -3), (hop2, -4), (turn, -2),
                      (attend0, -1), (weights2, -2), (hop1, -3), (weights0, -2), (spread_s1, -2), (weights1, -2),
                      (turn, -1), (hop2, -3), (weights2, -1), (weights1, -1), (spread_s1, -1), (hop1, -2),
                      (weights0, -1), (hop2, -2), (hop1, -1), (hop2, -1)), B)

        @block.scalar
        def _(act):
            act.dma_start(wv[:, :, :], Wv.rearrange("(c p) o -> p c o", p=P)).then_inc(ld_const, 16)
            act.dma_start(aw_all[:, :, :], aw.rearrange("(s d) o -> o s d", s=2).to_broadcast([P, 2, D]))\
                .then_inc(ld_const, 16)
            act.dma_start(bv_all[:, :], bv[None, :].to_broadcast([P, D])).then_inc(ld_const, 16)
            act.dma_start(ab_all[:, :], ab[None, :].to_broadcast([P, 1])).then_inc(ld_const, 16)
            for k in range(K):
                act.dma_start(W[:, k], Wk[k].rearrange("(c p) o -> p c o", p=P)).then_inc(ld_W, 16)
            act.dma_start(bk_all[:, :, :], bk[None, :, :].to_broadcast([P, K, D])).then_inc(ld_bk, 16)

            def keep_V1(g):
                done(act, weighed1, g)
                nc.scalar.activation(V1[:, g.slot], p1[:, :, :], ACT.Copy, scale=down[:, 1:2]).then_inc(V1_kept, 1)

            def row_of(name, g, row, slot_sems):
                if isinstance(g.number, int) and (name, g.number) in spread_rows:
                    n, bank = spread_rows[name, g.number]
                    act.wait_ge(row_spread, n + 1)
                    return bank
                landed(act, slot_sems, g, 1 if (name, g.slot) in spread_rows else 0)
                return row[:, g.slot, :]

            def tanh(g):
                row = row_of("s0", g, s0_all, s0_landed)
                for j in range(T):
                    last = nc.scalar.activation(E0[:, g.slot, j, :], row, ACT.Tanh,
                                                bias=s0[:, g.slot, j:j + 1])
                last.then_inc(tanh0, 1)

            def exp_0(g):
                done(act, lrelu0, g)
                nc.scalar.activation(E0[:, g.slot], E0[:, g.slot], ACT.Exp, scale=8.0).then_inc(exp0, 1)

            def sum_adj(g):
                landed(act, rows_landed, g)
                for t in range(T):
                    last = nc.scalar.activation(adj_rows[:, g.slot, t, :], adj_rows[:, g.slot, t, :], ACT.Copy,
                                                accum_out=adj_sum[:, g.slot, t:t + 1])
                last.then_inc(adj_summed, 1)

            def z(g):
                row = row_of("s1", g, s1_all, s1_landed)
                for j in range(T):
                    last = nc.scalar.activation(E1[:, g.slot, j, :], row, ACT.Identity,
                                                bias=s1[:, g.slot, 0, j:j + 1])
                last.then_inc(z1, 1)

            def exp_1(g):
                done(act, lrelu1, g)
                nc.scalar.activation(E1[:, g.slot], E1[:, g.slot], ACT.Exp).then_inc(exp1, 1)

            def high(g):
                done(act, X1_ready, g)
                nc.scalar.activation(Xhl[:, g.half, 0], X1[:, g.slot], ACT.Copy, scale=X_SCALE).then_inc(high_ready, 1)

            def keep_XT(g):
                done(act, turned, g)
                nc.scalar.activation(XT[:, g.half], pT[:, :, :, :, :], ACT.Copy).then_inc(XT_kept, 1)

            def keep_y(g):
                done(act, s0_ready, g)
                nc.scalar.activation(y[:, g.slot, :, 0:D], first_bank(g)[:, :, 0:D], ACT.Copy).then_inc(y_kept, 1)

            def keep_G(g):
                done(act, s1_ready, g)
                nc.scalar.activation(G[:, g.slot, :, 0:D], pX[:, :, 0:D], ACT.Copy, scale=down[:, 2:3])\
                    .then_inc(G_kept, 1)

            def finish(g):
                done(act, shift_ready, g)
                landed(act, stored, g, 1)
                for t in range(T):
                    last = nc.scalar.activation(res[:, g.slot, t, :], H[:, g.slot, t, :], ACT.Identity,
                                                bias=shift1[:, g.slot, t:t + 1], scale=rstd1[:, g.slot, t:t + 1])
                last.then_inc(res_ready, 1)
                done(act, res_ready, g)
                act.dma_start(out[g.number].rearrange("(p t) d -> p t d", t=T), res[:, g.slot])\
                    .then_inc(stored[g.slot], 16)

            def high_parts(parts):
                for src, k, lo, hi in parts:
                    last = nc.scalar.activation(Wh[:, :, lo:hi], src, ACT.Copy, scale=up[:, k:k + 1])
                last.then_inc(Wh_ready, 1)

            def high_W2():
                act.wait_ge(up_ready, 1)
                high_parts(weight_parts[:2])

            def high_W10():
                high_parts(weight_parts[2:])

            straight(((keep_y, 0), (keep_y, 1), (tanh, 0), (exp_0, 0), (keep_y, 2), (tanh, 1), (sum_adj, 0),
                      (keep_y, 3), (exp_0, 1), (high_W2, None), (sum_adj, 1), (high_W10, None), (tanh, 2),
                      (high, 0), (keep_XT, 0), (high, 1), (exp_0, 2), (keep_G, 0), (z, 0), (keep_XT, 1), (exp_1, 0),
                      (keep_V1, 0), (keep_G, 1), (sum_adj, 2)))
            steady(act, ((tanh, 1), (sum_adj, 1), (high, 2), (z, 3), (exp_0, 1), (keep_XT, 2), (keep_V1, 3), (exp_1, 3),
                         (keep_y, 0), (keep_G, 2), (finish, 4)))
            straight(((tanh, -1), (sum_adj, -1), (high, -2), (exp_0, -1), (z, -3), (keep_XT, -2), (exp_1, -3),
                      (keep_V1, -3), (keep_G, -2), (high, -1), (z, -2), (finish, -4), (keep_XT, -1),
                      (exp_1, -2), (keep_V1, -2), (keep_G, -1), (keep_V1, -1), (z, -1), (finish, -3), (exp_1, -1),
                      (finish, -2), (finish, -1)), B)
            for slot in range(SLOTS):
                act.wait_ge(stored[slot], 16 * BLOCKS)

        @block.gpsimd
        def _(pool):
            nc.gpsimd.memset(identity32[:, :], 0.0).then_inc(id_step, 1)
            nc.gpsimd.memset(minus_half[:, :], -0.5).then_inc(id_step, 1)
            nc.gpsimd.memset(eps[:, :], EPS).then_inc(id_step, 1)
            nc.gpsimd.memset(ones[:, :], 1.0).then_inc(id_step, 1)
            nc.gpsimd.memset(y[:, :, :, D:D + 1], 1.0).then_inc(id_step, 1)
            nc.gpsimd.memset(G[:, :, :, D:D + 1], 1.0).then_inc(id_step, 1)
            pool.wait_ge(id_step, 6)
            nc.gpsimd.affine_select(out=identity32[:, :], in_=identity32[:, :], compare_op=ALU.not_equal, fill=1.0,
                                    base=0, pattern=[[-1, P]], channel_multiplier=1).then_inc(id_step, 1)
            pool.wait_ge(id_step, 7)
            nc.gpsimd.tensor_copy(identity[:, :], identity32[:, :]).then_inc(identity_ready, 1)
            pool.wait_ge(ld_bk, 16)
            nc.gpsimd.tensor_tensor(b_sum[:, :], bk_all[:, 0, :], bk_all[:, 1, :], ALU.add).then_inc(b_sum_step, 1)
            pool.wait_ge(b_sum_step, 1)
            nc.gpsimd.tensor_tensor(b_sum[:, :], b_sum[:, :], bk_all[:, 2, :], ALU.add).then_inc(b_sum_step, 1)
            def inverse_std(g, mv, mv_ready, var, var_ready, rstd, rstd_ready):
                done(pool, mv_ready, g)
                nc.gpsimd.tensor_tensor(var[:, g.slot], mv[:, g.slot, :, 1], eps[:, :], ALU.add).then_inc(var_ready, 1)
                done(pool, var_ready, g)
                nc.gpsimd.tensor_tensor(rstd[:, g.slot], var[:, g.slot], minus_half[:, :], ALU.pow)\
                    .then_inc(rstd_ready, 1)

            def std0(g):
                inverse_std(g, mv0, mv0_ready, var0, var0_ready, rstd0, rstd0_ready)

            def times_adj0(g):
                done(pool, exp0, g)
                landed(pool, adj_landed, g)
                nc.gpsimd.tensor_tensor(E0[:, g.slot], E0[:, g.slot], adj_in[:, g.slot], ALU.mult).then_inc(E0_ready, 1)

            def times_adj1(g):
                done(pool, exp1, g)
                nc.gpsimd.tensor_tensor(E1[:, g.slot], E1[:, g.slot], adj_in[:, g.slot], ALU.mult).then_inc(E1_ready, 1)

            def std1(g):
                inverse_std(g, mv1, mv1_ready, var1, var1_ready, rstd1, rstd1_ready)

            def reduce_top():
                pool.wait_ge(top_ready, 1)
                nc.gpsimd.partition_all_reduce(top_all[:, :], top[:, :], P, bass.bass_isa.ReduceOp.max)\
                    .then_inc(top_reduced, 1)

            straight(((times_adj0, 0), (reduce_top, None), (times_adj0, 1), (std0, 0), (std0, 1), (times_adj0, 2), (times_adj1, 0)))
            steady(pool, ((std0, 2), (times_adj0, 1), (times_adj1, 3), (std1, 4)))
            straight(((std0, -2), (times_adj0, -1), (times_adj1, -3), (std0, -1), (std1, -4), (times_adj1, -2),
                      (std1, -3), (times_adj1, -1), (std1, -2), (std1, -1)), B)

        @block.vector
        def _(dve):
            dve.wait_ge(ld_w, 16)
            dve.wait_ge(ld_a, 16)
            for c in range(C):
                last = nc.vector.tensor_tensor_reduce(product[:, c, :], w_a[:, c, 0:D], a_all[:, :], 1.0, 0.0, ALU.mult,
                                                      ALU.add, w_a[:, c, D:D + 1])
            last.then_inc(wa_ready, 1)

            steps = [0]

            def chained(instruction):
                steps[0] += 1
                instruction.then_inc(const_step, 1)
                dve.wait_ge(const_step, steps[0])

            def constant_products():
                dve.wait_ge(ld_const, 16 * 4)
                for i in range(2):
                    for c in range(C):
                        nc.vector.tensor_tensor_reduce(product[:, C * (i + 1) + c, :], wv[:, c, :], aw_all[:, i, :],
                                                       1.0, 0.0, ALU.mult, ALU.add, v[:, c, i:i + 1])
                    last = nc.vector.tensor_tensor_reduce(product[:, 3 * C + i, :], bv_all[:, :], aw_all[:, i, :], 1.0,
                                                          0.0, ALU.mult, ALU.add, c_bias[:, i:i + 1])
                chained(last)

            def largest_entries():
                dve.wait_ge(ld_W, 16 * K)
                for k in range(K):
                    nc.vector.tensor_reduce(top[:, k:k + 1], W[:, k], AX.XY, ALU.max, apply_absolute_value=True)
                nc.vector.tensor_reduce(top[:, K:K + 1], v[:, :, :], AX.XY, ALU.max, apply_absolute_value=True)\
                    .then_inc(top_ready, 1)

            def bias_of_s1():
                chained(nc.vector.tensor_tensor(c_bias[:, 2:3], c_bias[:, 0:1], c_bias[:, 1:2], ALU.add))
                nc.vector.memset(s1_bias[:, :, 0], 0.0)
                for t in range(T):
                    last = nc.vector.tensor_tensor(s1_bias[:, t, 1:2], c_bias[:, 2:3], ab_all[:, :], ALU.add)
                chained(last)

            def scales():
                dve.wait_ge(top_reduced, 1)
                chained(nc.vector.tensor_scalar(top[:, :], top_all[:, :], 1e-30, None, ALU.max))
                chained(nc.vector.tensor_scalar(power[:, :].bitcast(U32), top[:, :].bitcast(U32), EXPONENT, None,
                                                ALU.bitwise_and))
                chained(nc.vector.reciprocal(inv_power[:, :], power[:, :]))
                nc.vector.tensor_scalar(up[:, :], inv_power[:, :], W_TOP, None, ALU.mult).then_inc(up_ready, 1)
                chained(nc.vector.tensor_scalar(down[:, :], power[:, :], 1.0 / (W_TOP * X_SCALE), None, ALU.mult))

            def low_parts(parts):
                for src, k, lo, hi in parts:
                    last = nc.vector.scalar_tensor_tensor(out=Wl[:, :, lo:hi], in0=src, scalar=up[:, k:k + 1],
                                                          in1=Wh[:, :, lo:hi], op0=ALU.mult, op1=ALU.subtract)
                last.then_inc(W_ready, 1)

            def low_W2():
                dve.wait_ge(up_ready, 1)
                dve.wait_ge(Wh_ready, 1)
                low_parts(weight_parts[:2])

            def low_W10():
                dve.wait_ge(Wh_ready, 2)
                low_parts(weight_parts[2:])
                dve.wait_ge(b_sum_step, 2)

            def residual0_first(g):
                residual0(g, first_bank(g))

            def residual0(g, bank=pY):
                done(dve, attended0, g)
                nc.vector.reciprocal(inv0[:, g.slot], bank[:, :, D]).then_inc(inv0_ready, 1)
                done(dve, inv0_ready, g)
                done(dve, adj_summed, g)
                nc.vector.tensor_tensor(r0[:, g.slot], adj_sum[:, g.slot], inv0[:, g.slot], ALU.mult).then_inc(r0_ready, 1)
                done(dve, r0_ready, g)
                landed(dve, x_landed, g)
                for t in range(T):
                    last = nc.vector.scalar_tensor_tensor(out=X1[:, g.slot, t, :], in0=bank[:, t, 0:D],
                                                          scalar=r0[:, g.slot, t:t + 1], in1=x_in[:, g.slot, t, :],
                                                          op0=ALU.mult, op1=ALU.add)
                last.then_inc(h_ready, 1)

            def stats0(g):
                done(dve, h_ready, g)
                statistics(g, X1, bn0, bn0_ready)

            def moments0(g):
                moments(g, bn0, bn0_ready, mv0, mv0_ready, waiter0)

            def statistics(g, rows, bn, bn_ready):
                for t in range(T):
                    last = nc.vector.bn_stats(bn[:, g.slot, t, :], rows[:, g.slot, t, :])
                last.then_inc(bn_ready, 1)

            def moments(g, bn, bn_ready, mv, mv_ready, waiter):
                done(dve, bn_ready, g)
                nc.vector.memset(waiter[:, g.slot], 0.0)
                for t in range(T):
                    last = nc.vector.bn_aggr(mv[:, g.slot, t, :], bn[:, g.slot, t, :])
                last.then_inc(mv_ready, 1)

            def add_V1(g):
                done(dve, hopped1, g)
                nc.vector.tensor_scalar(den1[:, g.slot], pX[:, :, D], 1e-12, None, ALU.add).then_inc(den1_ready, 1)
                done(dve, den1_ready, g)
                nc.vector.reciprocal(r1[:, g.slot], den1[:, g.slot]).then_inc(r1_ready, 1)
                done(dve, r1_ready, g)
                done(dve, V1_kept, g)
                for t in range(T):
                    last = nc.vector.scalar_tensor_tensor(out=U[:, g.slot, t, :], in0=pX[:, t, 0:D],
                                                          scalar=r1[:, g.slot, t:t + 1], in1=V1[:, g.slot, t, :],
                                                          op0=ALU.mult, op1=ALU.add)
                last.then_inc(U_ready, 1)

            def norm0(g):
                done(dve, rstd0_ready, g)
                for t in range(T):
                    last = nc.vector.tensor_scalar(X1[:, g.slot, t, :], X1[:, g.slot, t, :], mv0[:, g.slot, t, 0:1],
                                                   rstd0[:, g.slot, t:t + 1], ALU.subtract, ALU.mult)
                last.then_inc(X1_ready, 1)

            def leaky0(g):
                done(dve, tanh0, g)
                nc.vector.scalar_tensor_tensor(out=E0[:, g.slot], in0=E0[:, g.slot], scalar=0.1, in1=E0[:, g.slot],
                                               op0=ALU.mult, op1=ALU.max).then_inc(lrelu0, 1)

            def leaky1(g):
                done(dve, z1, g)
                nc.vector.scalar_tensor_tensor(out=E1[:, g.slot], in0=E1[:, g.slot], scalar=0.2, in1=E1[:, g.slot],
                                               op0=ALU.mult, op1=ALU.max).then_inc(lrelu1, 1)

            def low(g):
                done(dve, high_ready, g)
                nc.vector.scalar_tensor_tensor(out=Xhl[:, g.half, 1], in0=X1[:, g.slot], scalar=X_SCALE,
                                               in1=Xhl[:, g.half, 0], op0=ALU.mult, op1=ALU.subtract)\
                    .then_inc(low_ready, 1)

            def keep_V0(g):
                done(dve, weighed0, g)
                nc.vector.scalar_tensor_tensor(out=V0[:, g.slot], in0=p0[:, :, :], scalar=down[:, 0:1],
                                               in1=b_sum[:, None, :].to_broadcast([P, T, D]),
                                               op0=ALU.mult, op1=ALU.add).then_inc(V0_kept, 1)

            def residual1(g):
                done(dve, hopped2, g)
                done(dve, V0_kept, g)
                for t in range(T):
                    last = nc.vector.scalar_tensor_tensor(out=H[:, g.slot, t, :], in0=pU[:, t, :],
                                                          scalar=r1[:, g.slot, t:t + 1], in1=V0[:, g.slot, t, :],
                                                          op0=ALU.mult, op1=ALU.add)
                last.then_inc(H_ready, 1)

            def relu_add(g):
                done(dve, H_ready, g)
                nc.vector.scalar_tensor_tensor(out=H[:, g.slot], in0=H[:, g.slot], scalar=0.0, in1=X1[:, g.slot],
                                               op0=ALU.max, op1=ALU.add).then_inc(relu_added, 1)

            def stats1(g):
                done(dve, relu_added, g)
                statistics(g, H, bn1, bn1_ready)

            def moments1(g):
                moments(g, bn1, bn1_ready, mv1, mv1_ready, waiter1)

            def shift(g):
                done(dve, rstd1_ready, g)
                nc.vector.scalar_tensor_tensor(out=shift1[:, g.slot], in0=mv1[:, g.slot, :, 0], scalar=-1.0,
                                               in1=rstd1[:, g.slot], op0=ALU.mult, op1=ALU.mult).then_inc(shift_ready, 1)

            def s0_column(g):
                done(dve, embedded, g)
                nc.vector.tensor_scalar(s0[:, g.slot], first_bank(g)[:, :, D], 0.125, None, ALU.mult).then_inc(s0_ready, 1)

            def s1_columns(g):
                done(dve, weighed2, g)
                nc.vector.scalar_tensor_tensor(out=s1[:, g.slot].rearrange("p k t -> p t k"), in0=pX[:, :, D:D + 2],
                                               scalar=down[:, 3:4], in1=s1_bias[:, :, :],
                                               op0=ALU.mult, op1=ALU.add).then_inc(s1_ready, 1)

            def make_diagonal(key, column):
                n, _ = spread_rows[key]
                dve.wait_ge(id_step, 7)
                for t in range(T):
                    last = nc.vector.tensor_scalar(diagonal[:, n, t, :], identity32[:, :], column[:, t:t + 1], None,
                                                   ALU.mult)
                last.then_inc(diagonal_ready, 1)

            def diagonal_s0(g):
                done(dve, s0_ready, g)
                make_diagonal(("s0", g.number), s0[:, g.slot])

            def diagonal_s1(g):
                done(dve, s1_ready, g)
                make_diagonal(("s1", g.number), s1[:, g.slot, 1])

            straight(((constant_products, None), (s0_column, 0), (diagonal_s0, 0), (s0_column, 1), (diagonal_s0, 1),
                      (leaky0, 0), (s0_column, 2), (largest_entries, None), (leaky0, 1), (s0_column, 3),
                      (bias_of_s1, None), (scales, None), (residual0_first, 0), (stats0, 0), (moments0, 0),
                      (residual0_first, 1), (norm0, 0), (stats0, 1), (low, 0), (moments0, 1), (low_W2, None),
                      (norm0, 1), (low, 1), (leaky0, 2), (low_W10, None), (s1_columns, 0), (diagonal_s1, 0),
                      (keep_V0, 0), (leaky1, 0), (s1_columns, 1)))
            steady(dve, ((residual0, 2), (stats0, 2), (moments0, 2), (add_V1, 4), (norm0, 2), (leaky0, 1), (low, 2), (leaky1, 3), (keep_V0, 3),
                         (residual1, 4), (s0_column, 0), (relu_add, 4), (stats1, 4), (s1_columns, 2), (moments1, 4), (shift, 4)))
            straight(((residual0, -2), (stats0, -2), (moments0, -2), (add_V1, -4), (norm0, -2), (leaky0, -1),
                      (low, -2), (leaky1, -3), (keep_V0, -3), (residual1, -4), (relu_add, -4), (residual0, -1),
                      (stats0, -1), (s1_columns, -2), (diagonal_s1, -2), (moments0, -1), (stats1, -4), (moments1, -4),
                      (norm0, -1), (low, -1), (shift, -4), (add_V1, -3), (leaky1, -2), (keep_V0, -2),
                      (residual1, -3), (relu_add, -3), (stats1, -3), (s1_columns, -1), (diagonal_s1, -1),
                      (moments1, -3), (leaky1, -1), (shift, -3), (add_V1, -2), (keep_V0, -1), (residual1, -2),
                      (relu_add, -2), (stats1, -2), (moments1, -2), (add_V1, -1), (shift, -2),
                      (residual1, -1), (relu_add, -1), (stats1, -1), (moments1, -1), (shift, -1)), B)


_ORDER = ["x", "xT", "adj", "adjT", "w", "a", "Wv", "bv", "aw", "ab", "Wk", "bk"]


def kernel(x, adj, L0_gnn_w, L0_gnn_a, L1_gnn_Wv, L1_gnn_bv, L1_gnn_aw, L1_gnn_ab, L1_gnn_Wk, L1_gnn_bk):
    import concourse.bacc as bacc
    from concourse.bass_utils import run_bass_kernel_spmd

    x, adj = np.asarray(x), np.asarray(adj)
    inputs = {
        "x": x, "xT": x.transpose(0, 2, 1), "adj": adj, "adjT": adj.transpose(0, 2, 1), "w": L0_gnn_w, "a": L0_gnn_a,
        "Wv": L1_gnn_Wv, "bv": L1_gnn_bv, "aw": L1_gnn_aw, "ab": L1_gnn_ab, "Wk": L1_gnn_Wk, "bk": L1_gnn_bk,
    }
    nc = bacc.Bacc("TRN2", target_bir_lowering=False, num_devices=1)
    arrays, args = {}, []
    for name in _ORDER:
        array = np.ascontiguousarray(np.asarray(inputs[name]))
        arrays[f"in_{name}"] = array
        args.append(nc.dram_tensor(f"in_{name}", array.shape, mybir.dt.from_np(array.dtype), kind="ExternalInput").ap())
    result = nc.dram_tensor("result", x.shape, F32, kind="ExternalOutput").ap()
    graph_layers_kernel(nc, *args, result)
    run = run_bass_kernel_spmd(nc, [arrays], core_ids=[0])
    return run.results[0]["result"]
```

```python
from contextlib import ExitStack

import numpy as np

import concourse.bass as bass
from concourse import mybir

F32 = mybir.dt.float32
F16 = mybir.dt.float16
U32 = mybir.dt.uint32
ALU = mybir.AluOpType
ACT = mybir.ActivationFunctionType
AX = mybir.AxisListType

P = 128
SLOTS = 4
EPS = 1e-5
X_SCALE = 2048.0
W_TOP = 2.0 ** 14
EXPONENT = 0x7F800000


def graph_layers_kernel(nc, x, xT, adj, adjT, w, a, Wv, bv, aw, ab, Wk, bk, out):
    B, N, D = x.shape
    K = Wk.shape[0]
    T = N // P
    C = D // P
    assert N == D == 2 * P and K == 3 and B % SLOTS == 0
    BLOCKS = B // SLOTS

    s0_row = nc.dram_tensor("s0_row", [B, N], F32, kind="Internal").ap()
    s1_row = nc.dram_tensor("s1_row", [B, N], F32, kind="Internal").ap()

    with ExitStack() as ctx:
        def sb(name, shape, dt=F32):
            return ctx.enter_context(nc.sbuf_tensor(name, shape, dt))

        def ps(name, shape, dt=F32):
            return ctx.enter_context(nc.psum_tensor(name, shape, dt))

        def sem(name):
            return ctx.enter_context(nc.semaphore(name))

        def sems(name):
            return [sem(f"{name}{i}") for i in range(SLOTS)]

        w_a = sb("w_a", [P, C, D + 1])
        a_all = sb("a_all", [P, D])
        wv = sb("wv", [P, C, D])
        aw_all = sb("aw_all", [P, 2, D])
        bv_all = sb("bv_all", [P, D])
        ab_all = sb("ab_all", [P, 1])
        bk_all = sb("bk_all", [P, K, D])
        b_sum = sb("b_sum", [P, D])
        W = sb("W", [P, K, C, D])
        v = sb("v", [P, C, 2])
        Wh = sb("Wh", [P, C, K * D + 2], F16)
        Wl = sb("Wl", [P, C, K * D + 2], F16)
        product = sb("product", [P, 4 * C, D])
        top = sb("top", [P, K + 1])
        top_all = sb("top_all", [P, K + 1])
        power = sb("power", [P, K + 1])
        inv_power = sb("inv_power", [P, K + 1])
        up = sb("up", [P, K + 1])
        down = sb("down", [P, K + 1])
        c_bias = sb("c_bias", [P, 3])
        s1_bias = sb("s1_bias", [P, T, 2])
        identity32 = sb("identity32", [P, P])
        identity = sb("identity", [P, P], F16)
        ones = sb("ones", [P, P])
        minus_half = sb("minus_half", [P, T])
        eps = sb("eps", [P, T])

        weight_parts = ((W[:, 2], 2, 0, D), (v[:, :, :], 3, D, D + 2), (W[:, 1], 1, D + 2, 2 * D + 2),
                        (W[:, 0], 0, 2 * D + 2, 3 * D + 2))

        diagonal = sb("diagonal", [P, 6, T, P])

        xT_in = sb("xT_in", [P, SLOTS, C, N])
        x_in = sb("x_in", [P, SLOTS, T, D])
        adj_in = sb("adj_in", [P, SLOTS, T, N])
        y = sb("y", [P, SLOTS, T, D + 1])
        s0 = sb("s0", [P, SLOTS, T])
        s0_all = sb("s0_all", [P, SLOTS, N])
        E0 = sb("E0", [P, SLOTS, T, N])
        adj_rows = sb("adj_rows", [P, SLOTS, T, N])
        adj_sum = sb("adj_sum", [P, SLOTS, T])
        inv0 = sb("inv0", [P, SLOTS, T])
        r0 = sb("r0", [P, SLOTS, T])
        X1 = sb("X1", [P, SLOTS, T, D])
        bn0 = sb("bn0", [P, SLOTS, T, 6])
        mv0 = sb("mv0", [P, SLOTS, T, 2])
        var0 = sb("var0", [P, SLOTS, T])
        rstd0 = sb("rstd0", [P, SLOTS, T])
        waiter0 = sb("waiter0", [P, SLOTS, 1])
        waiter1 = sb("waiter1", [P, SLOTS, 1])
        Xhl = sb("Xhl", [P, 2, 2, T, D], F16)
        XT = sb("XT", [P, 2, 2, C, T, P], F16)
        G = sb("G", [P, SLOTS, T, D + 1])
        V1 = sb("V1", [P, SLOTS, T, D])
        V0 = sb("V0", [P, SLOTS, T, D])
        s1 = sb("s1", [P, SLOTS, 2, T])
        s1_all = sb("s1_all", [P, SLOTS, N])
        E1 = sb("E1", [P, SLOTS, T, N])
        den1 = sb("den1", [P, SLOTS, T])
        r1 = sb("r1", [P, SLOTS, T])
        U = sb("U", [P, SLOTS, T, D])
        H = sb("H", [P, SLOTS, T, D])
        bn1 = sb("bn1", [P, SLOTS, T, 6])
        mv1 = sb("mv1", [P, SLOTS, T, 2])
        var1 = sb("var1", [P, SLOTS, T])
        rstd1 = sb("rstd1", [P, SLOTS, T])
        shift1 = sb("shift1", [P, SLOTS, T])
        res = sb("res", [P, SLOTS, T, D])

        pY = ps("pY", [P, T, 512])
        pX = ps("pX", [P, T, 512])
        p1 = ps("p1", [P, T, D])
        p0 = ps("p0", [P, T, D])
        pU = ps("pU", [P, T, D])
        pT = ps("pT", [P, 2, C, T, P], F16)

        spread_rows = {("s0", 0): (0, p0[:, 0, :]), ("s0", 1): (1, p1[:, 0, :]), ("s0", 2): (2, p0[:, 1, :]),
                       ("s1", 0): (3, pU[:, 0, :]),
                       ("s1", B - 2): (4, pY[:, 1, 0:N]), ("s1", B - 1): (5, pY[:, 0, 0:N])}
        S0_SPREAD, S1_SPREAD = 3, 1

        ld_w, ld_a, ld_const, ld_W = sem("ld_w"), sem("ld_a"), sem("ld_const"), sem("ld_W")
        ld_bk = sem("ld_bk")
        const_step = sem("const_step")
        id_step, identity_ready = sem("id_step"), sem("identity_ready")
        b_sum_step, top_ready, top_reduced = sem("b_sum_step"), sem("top_ready"), sem("top_reduced")
        wa_ready, up_ready, Wh_ready, W_ready = sem("wa_ready"), sem("up_ready"), sem("Wh_ready"), sem("W_ready")
        xT_landed, x_landed = sems("xT_landed"), sems("x_landed")
        adj_landed, rows_landed = sems("adj_landed"), sems("rows_landed")
        s0_sent, s1_sent = sem("s0_sent"), sem("s1_sent")
        s0_landed, s1_landed, stored = sems("s0_landed"), sems("s1_landed"), sems("stored")
        embedded, y_kept, s0_ready = sem("embedded"), sem("y_kept"), sem("s0_ready")
        tanh0, lrelu0, exp0, E0_ready, adj_summed = (
            sem("tanh0"), sem("lrelu0"), sem("exp0"), sem("E0_ready"), sem("adj_summed"))
        attended0, inv0_ready, r0_ready, h_ready = (
            sem("attended0"), sem("inv0_ready"), sem("r0_ready"), sem("h_ready"))
        bn0_ready, mv0_ready, var0_ready, rstd0_ready, X1_ready = (
            sem("bn0_ready"), sem("mv0_ready"), sem("var0_ready"), sem("rstd0_ready"), sem("X1_ready"))
        high_ready, low_ready, turned, XT_kept = (
            sem("high_ready"), sem("low_ready"), sem("turned"), sem("XT_kept"))
        weighed2, weighed1, weighed0 = sem("weighed2"), sem("weighed1"), sem("weighed0")
        G_kept, V1_kept, V0_kept, s1_ready = sem("G_kept"), sem("V1_kept"), sem("V0_kept"), sem("s1_ready")
        z1, lrelu1, exp1, E1_ready = sem("z1"), sem("lrelu1"), sem("exp1"), sem("E1_ready")
        hopped1, den1_ready, r1_ready, U_ready = (
            sem("hopped1"), sem("den1_ready"), sem("r1_ready"), sem("U_ready"))
        hopped2, H_ready, relu_added = sem("hopped2"), sem("H_ready"), sem("relu_added")
        bn1_ready, mv1_ready, var1_ready, rstd1_ready, res_ready = (
            sem("bn1_ready"), sem("mv1_ready"), sem("var1_ready"), sem("rstd1_ready"), sem("res_ready"))
        shift_ready = sem("shift_ready")
        last_res_ready = sem("last_res_ready")
        diagonal_ready, row_spread = sem("diagonal_ready"), sem("row_spread")

        block = ctx.enter_context(nc.Block())

        class Graph:

            def __init__(self, q, u, back):
                self.q, self.slot = q + (u - back) // SLOTS, (u - back) % SLOTS
                self.half = self.slot % 2
                self.number = self.q * SLOTS + self.slot

        def done(eng, sem_, g, ahead=0):
            n = g.number + ahead + 1
            if isinstance(n, int):
                n = min(n, B)
                if n <= 0:
                    return
            eng.wait_ge(sem_, n)

        def landed(eng, slot_sems, g, ago=0):
            n = 16 * (g.q + 1 - ago)
            if isinstance(n, int) and n <= 0:
                return
            eng.wait_ge(slot_sems[g.slot], n)

        def steady(eng, steps):
            with eng.Fori(1, BLOCKS) as q:
                for u in range(SLOTS):
                    for step, back in steps:
                        step(Graph(q, u, back))

        def first_bank(g):
            return pX if isinstance(g.q, int) and g.q == 0 and g.number % 2 else pY

        def straight(steps, base=0):
            for step, n in steps:
                if n is None:
                    step()
                else:
                    step(Graph((base + n) // SLOTS, (base + n) % SLOTS, 0))

        @block.sync
        def _(sp):
            sp.dma_start(w_a[:, :, 0:D], w.rearrange("(p c) o -> p c o", c=C)).then_inc(ld_w, 16)
            sp.dma_start(a_all[:, :], a[None, :].to_broadcast([P, D])).then_inc(ld_a, 16)

            def load_xT(g):
                done(sp, embedded, g, -SLOTS)
                sp.dma_start(xT_in[:, g.slot], xT[g.number].rearrange("(p c) n -> p c n", c=C))\
                    .then_inc(xT_landed[g.slot], 16)

            def load_x(g):
                done(sp, h_ready, g, -SLOTS)
                sp.dma_start(x_in[:, g.slot], x[g.number].rearrange("(p t) d -> p t d", t=T))\
                    .then_inc(x_landed[g.slot], 16)

            def load_adj(g):
                done(sp, E1_ready, g, -SLOTS)
                sp.dma_start(adj_in[:, g.slot], adjT[g.number].rearrange("(p t) n -> p t n", t=T))\
                    .then_inc(adj_landed[g.slot], 16)

            def load_rows(g):
                done(sp, adj_summed, g, -SLOTS)
                sp.dma_start(adj_rows[:, g.slot], adj[g.number].rearrange("(p t) n -> p t n", t=T))\
                    .then_inc(rows_landed[g.slot], 16)

            def send_s0(g):
                done(sp, s0_ready, g)
                sp.dma_start(s0_row[g.number].rearrange("(p t) -> p t", t=T), s0[:, g.slot]).then_inc(s0_sent, 16)

            def spread_s0(g):
                sp.wait_ge(s0_sent, (g.number + 1 - S0_SPREAD) * 16)
                sp.dma_start(s0_all[:, g.slot], s0_row[g.number][None, :].to_broadcast([P, N]))\
                    .then_inc(s0_landed[g.slot], 16)

            def send_s1(g):
                done(sp, s1_ready, g)
                sp.dma_start(s1_row[g.number].rearrange("(p t) -> p t", t=T), s1[:, g.slot, 1]).then_inc(s1_sent, 16)

            def spread_s1(g):
                sp.wait_ge(s1_sent, (g.number + 1 - S1_SPREAD) * 16)
                sp.dma_start(s1_all[:, g.slot], s1_row[g.number][None, :].to_broadcast([P, N]))\
                    .then_inc(s1_landed[g.slot], 16)

            straight(((load_xT, 0), (load_xT, 2), (load_xT, 1), (load_xT, 3), (load_x, 0), (load_adj, 0),
                      (load_adj, 1), (load_adj, 2), (load_rows, 0), (load_x, 2),
                      (load_rows, 2), (load_x, 1), (load_rows, 1), (load_rows, 3),
                      (load_adj, 3), (load_x, 3)))
            steady(sp, ((send_s0, 1), (load_xT, 0), (send_s1, 3), (spread_s0, 1), (load_x, 0), (load_adj, 0),
                        (spread_s1, 3), (load_rows, 0)))
            straight(((send_s0, -1), (spread_s0, -1), (send_s1, -3), (spread_s1, -3)), B)

        @block.tensor
        def _(pe):
            def embed(g, kept=-1, attended=-2):
                landed(pe, xT_landed, g)
                done(pe, y_kept, g, kept)
                done(pe, h_ready, g, attended)
                bank = first_bank(g)
                for t in range(T):
                    for c in range(C):
                        last = nc.tensor.matmul(bank[:, t, 0:D + 1], xT_in[:, g.slot, c, t:N:T], w_a[:, c, :],
                                                start=(c == 0), stop=(c == C - 1))
                last.then_inc(embedded, 1)

            def attend0(g, kept=1, attended=-1):
                done(pe, E0_ready, g)
                done(pe, y_kept, g, kept)
                done(pe, h_ready, g, attended)
                bank = first_bank(g) if attended < -1 else pY
                for t in range(T):
                    for j in range(T):
                        last = nc.tensor.matmul(bank[:, t, 0:D + 1], E0[:, g.slot, j, t:N:T], y[:, g.slot, j, :],
                                                start=(j == 0), stop=(j == T - 1))
                last.then_inc(attended0, 1)

            def turn(g):
                done(pe, high_ready, g)
                done(pe, low_ready, g)
                done(pe, XT_kept, g, -1)
                for part in range(2):
                    for c in range(C):
                        for t in range(T):
                            last = nc.tensor.transpose(pT[:, part, c, t, :],
                                                       Xhl[:, g.half, part, t, c * P:(c + 1) * P], identity[:, :])
                last.then_inc(turned, 1)

            def weigh(g, bank, lo, hi, signal):
                for t in range(T):
                    n = 0
                    for c in range(C):
                        for xp, wp in ((0, Wh), (0, Wl), (1, Wh)):
                            last = nc.tensor.matmul(bank[:, t, 0:hi - lo], XT[:, g.half, xp, c, t, :],
                                                    wp[:, c, lo:hi], start=(n == 0), stop=(n == 3 * C - 1))
                            n += 1
                last.then_inc(signal, 1)

            def weights2(g):
                done(pe, XT_kept, g)
                done(pe, G_kept, g, -1)
                done(pe, U_ready, g, -2)
                weigh(g, pX, 0, D + 2, weighed2)

            def weights1(g):
                done(pe, V1_kept, g, -1)
                weigh(g, p1, D + 2, 2 * D + 2, weighed1)

            def weights0(g):
                done(pe, V0_kept, g, -1)
                weigh(g, p0, 2 * D + 2, 3 * D + 2, weighed0)

            def hop1(g):
                done(pe, E1_ready, g)
                done(pe, G_kept, g, 1)
                done(pe, U_ready, g, -1)
                for t in range(T):
                    for j in range(T):
                        last = nc.tensor.matmul(pX[:, t, 0:D + 1], E1[:, g.slot, j, t:N:T], G[:, g.slot, j, :],
                                                start=(j == 0), stop=(j == T - 1))
                last.then_inc(hopped1, 1)

            def hop2_last(g):
                hop2(g, p1)

            def hop2(g, bank=pU):
                done(pe, U_ready, g)
                if bank is pU:
                    done(pe, H_ready, g, -1)
                for t in range(T):
                    for j in range(T):
                        last = nc.tensor.matmul(bank[:, t, :], E1[:, g.slot, j, t:N:T], U[:, g.slot, j, :],
                                                start=(j == 0), stop=(j == T - 1))
                last.then_inc(hopped2, 1)

            def embed_first(g):
                embed(g, kept=-2, attended=-SLOTS)

            def attend0_first(g):
                attend0(g, kept=min(2, SLOTS - 1 - g.number), attended=-2)

            def spread_row(key):
                n, bank = spread_rows[key]
                pe.wait_ge(diagonal_ready, n + 1)
                for t in range(T):
                    last = nc.tensor.matmul(bank[:, t:N:T], ones[:, :], diagonal[:, n, t, :], start=True, stop=True)
                last.then_inc(row_spread, 1)

            def spread_s0(g):
                if g.number == 2:
                    pe.wait_ge(tanh0, 1)
                spread_row(("s0", g.number))

            def spread_s1(g):
                if g.number == B - 2:
                    pe.wait_ge(h_ready, B)
                spread_row(("s1", g.number))

            def need_W2():
                pe.wait_ge(W_ready, 1)
                pe.wait_ge(h_ready, 2)

            def need_W():
                pe.wait_ge(W_ready, 2)

            def stay_warm(products):
                for _ in range(products):
                    nc.tensor.matmul(pU[:, 0, 0:P], ones[:, :], ones[:, :], start=True, stop=True)

            pe.wait_ge(id_step, 4)
            stay_warm(12)
            pe.wait_ge(wa_ready, 1)
            straight(((embed_first, 0), (embed_first, 1), (spread_s0, 0), (embed_first, 2), (spread_s0, 1),
                      (embed_first, 3), (spread_s0, 2), (attend0_first, 0), (attend0_first, 1)))
            stay_warm(12)
            pe.wait_ge(identity_ready, 1)
            straight(((turn, 0), (attend0_first, 2), (need_W2, None), (weights2, 0), (need_W, None), (weights0, 0),
                      (spread_s1, 0), (turn, 1), (weights1, 0), (weights2, 1)))
            steady(pe, ((hop1, 4), (weights0, 3), (weights1, 3), (hop2, 4), (turn, 2), (embed, 0), (weights2, 2),
                        (attend0, 1)))
            straight(((hop1, -4), (weights0, -3), (weights1, -3), (hop2, -4), (turn, -2), (attend0, -1),
                      (weights2, -2), (weights0, -2), (hop1, -3), (spread_s1, -2), (turn, -1),
                      (weights1, -2), (weights2, -1), (weights1, -1), (spread_s1, -1),
                      (hop2, -3), (hop1, -2), (weights0, -1), (hop1, -1), (hop2, -2),
                      (hop2_last, -1)), B)

        @block.scalar
        def _(act):
            act.dma_start(wv[:, :, :], Wv.rearrange("(c p) o -> p c o", p=P)).then_inc(ld_const, 16)
            act.dma_start(aw_all[:, :, :], aw.rearrange("(s d) o -> o s d", s=2).to_broadcast([P, 2, D]))\
                .then_inc(ld_const, 16)
            act.dma_start(bv_all[:, :], bv[None, :].to_broadcast([P, D])).then_inc(ld_const, 16)
            act.dma_start(ab_all[:, :], ab[None, :].to_broadcast([P, 1])).then_inc(ld_const, 16)
            act.dma_start(W.rearrange("p k c o -> p (k c) o"),
                          Wk.rearrange("k (c p) o -> p (k c) o", p=P)).then_inc(ld_W, 16)
            act.dma_start(bk_all[:, :, :], bk[None, :, :].to_broadcast([P, K, D])).then_inc(ld_bk, 16)

            def keep_V1(g):
                done(act, weighed1, g)
                nc.scalar.activation(V1[:, g.slot], p1[:, :, :], ACT.Copy, scale=down[:, 1:2]).then_inc(V1_kept, 1)

            def row_of(name, g, row, slot_sems):
                if isinstance(g.number, int) and (name, g.number) in spread_rows:
                    n, bank = spread_rows[name, g.number]
                    act.wait_ge(row_spread, n + 1)
                    return bank
                landed(act, slot_sems, g, 1 if (name, g.slot) in spread_rows else 0)
                return row[:, g.slot, :]

            def tanh(g):
                row = row_of("s0", g, s0_all, s0_landed)
                for j in range(T):
                    last = nc.scalar.activation(E0[:, g.slot, j, :], row, ACT.Tanh,
                                                bias=s0[:, g.slot, j:j + 1])
                last.then_inc(tanh0, 1)

            def exp_0(g):
                done(act, lrelu0, g)
                nc.scalar.activation(E0[:, g.slot], E0[:, g.slot], ACT.Exp, scale=8.0).then_inc(exp0, 1)

            def sum_adj(g):
                landed(act, rows_landed, g)
                for t in range(T):
                    last = nc.scalar.activation(adj_rows[:, g.slot, t, :], adj_rows[:, g.slot, t, :], ACT.Copy,
                                                accum_out=adj_sum[:, g.slot, t:t + 1])
                last.then_inc(adj_summed, 1)

            def z(g):
                row = row_of("s1", g, s1_all, s1_landed)
                for j in range(T):
                    last = nc.scalar.activation(E1[:, g.slot, j, :], row, ACT.Identity,
                                                bias=s1[:, g.slot, 0, j:j + 1])
                last.then_inc(z1, 1)

            def exp_1(g):
                done(act, lrelu1, g)
                nc.scalar.activation(E1[:, g.slot], E1[:, g.slot], ACT.Exp).then_inc(exp1, 1)

            def high(g):
                done(act, X1_ready, g)
                nc.scalar.activation(Xhl[:, g.half, 0], X1[:, g.slot], ACT.Copy, scale=X_SCALE).then_inc(high_ready, 1)

            def keep_XT(g):
                done(act, turned, g)
                nc.scalar.activation(XT[:, g.half], pT[:, :, :, :, :], ACT.Copy).then_inc(XT_kept, 1)

            def keep_y(g):
                done(act, s0_ready, g)
                nc.scalar.activation(y[:, g.slot, :, 0:D], first_bank(g)[:, :, 0:D], ACT.Copy).then_inc(y_kept, 1)

            def keep_G(g):
                done(act, s1_ready, g)
                nc.scalar.activation(G[:, g.slot, :, 0:D], pX[:, :, 0:D], ACT.Copy, scale=down[:, 2:3])\
                    .then_inc(G_kept, 1)

            def finish(g):
                done(act, shift_ready, g)
                landed(act, stored, g, 1)
                for t in range(T):
                    last = nc.scalar.activation(res[:, g.slot, t, :], H[:, g.slot, t, :], ACT.Identity,
                                                bias=shift1[:, g.slot, t:t + 1], scale=rstd1[:, g.slot, t:t + 1])
                last.then_inc(res_ready, 1)
                done(act, res_ready, g)
                store(g)

            def store_last(g):
                act.wait_ge(last_res_ready, 1)
                store(g)

            def store(g):
                act.dma_start(out[g.number].rearrange("(p t) d -> p t d", t=T), res[:, g.slot])\
                    .then_inc(stored[g.slot], 16)

            def high_parts(parts):
                for src, k, lo, hi in parts:
                    last = nc.scalar.activation(Wh[:, :, lo:hi], src, ACT.Copy, scale=up[:, k:k + 1])
                last.then_inc(Wh_ready, 1)

            def high_W2():
                act.wait_ge(up_ready, 1)
                high_parts(weight_parts[:2])

            def high_W10():
                high_parts(weight_parts[2:])

            straight(((keep_y, 0), (keep_y, 1), (tanh, 0), (exp_0, 0), (tanh, 1), (keep_y, 2), (exp_0, 1),
                      (sum_adj, 0), (keep_y, 3), (tanh, 2), (sum_adj, 1), (exp_0, 2),
                      (high_W2, None), (high, 0), (high_W10, None), (keep_XT, 0),
                      (sum_adj, 2), (high, 1), (keep_G, 0), (z, 0), (keep_XT, 1), (exp_1, 0),
                      (keep_V1, 0), (keep_G, 1)))
            steady(act, ((tanh, 1), (sum_adj, 1), (high, 2), (z, 3), (exp_0, 1), (keep_XT, 2), (keep_V1, 3), (exp_1, 3),
                         (keep_y, 0), (keep_G, 2), (finish, 4)))
            straight(((sum_adj, -1), (tanh, -1), (high, -2), (exp_0, -1), (keep_XT, -2), (z, -3), (keep_V1, -3),
                      (exp_1, -3), (keep_G, -2), (high, -1), (z, -2), (keep_XT, -1),
                      (keep_V1, -2), (exp_1, -2), (finish, -4), (keep_G, -1), (keep_V1, -1), (z, -1),
                      (exp_1, -1), (finish, -3), (finish, -2), (store_last, -1)), B)
            for slot in range(SLOTS):
                act.wait_ge(stored[slot], 16 * BLOCKS)

        @block.gpsimd
        def _(pool):
            nc.gpsimd.memset(identity32[:, :], 0.0).then_inc(id_step, 1)
            nc.gpsimd.memset(minus_half[:, :], -0.5).then_inc(id_step, 1)
            nc.gpsimd.memset(eps[:, :], EPS).then_inc(id_step, 1)
            nc.gpsimd.memset(ones[:, :], 1.0).then_inc(id_step, 1)
            nc.gpsimd.memset(y[:, :, :, D:D + 1], 1.0).then_inc(id_step, 1)
            nc.gpsimd.memset(G[:, :, :, D:D + 1], 1.0).then_inc(id_step, 1)
            pool.wait_ge(id_step, 6)
            nc.gpsimd.affine_select(out=identity32[:, :], in_=identity32[:, :], compare_op=ALU.not_equal, fill=1.0,
                                    base=0, pattern=[[-1, P]], channel_multiplier=1).then_inc(id_step, 1)
            pool.wait_ge(id_step, 7)
            nc.gpsimd.tensor_copy(identity[:, :], identity32[:, :]).then_inc(identity_ready, 1)
            pool.wait_ge(ld_bk, 16)
            nc.gpsimd.tensor_tensor(b_sum[:, :], bk_all[:, 0, :], bk_all[:, 1, :], ALU.add).then_inc(b_sum_step, 1)
            pool.wait_ge(b_sum_step, 1)
            nc.gpsimd.tensor_tensor(b_sum[:, :], b_sum[:, :], bk_all[:, 2, :], ALU.add).then_inc(b_sum_step, 1)
            def inverse_std(g, mv, mv_ready, var, var_ready, rstd, rstd_ready):
                done(pool, mv_ready, g)
                nc.gpsimd.tensor_tensor(var[:, g.slot], mv[:, g.slot, :, 1], eps[:, :], ALU.add).then_inc(var_ready, 1)
                done(pool, var_ready, g)
                nc.gpsimd.tensor_tensor(rstd[:, g.slot], var[:, g.slot], minus_half[:, :], ALU.pow)\
                    .then_inc(rstd_ready, 1)

            def std0(g):
                inverse_std(g, mv0, mv0_ready, var0, var0_ready, rstd0, rstd0_ready)

            def times_adj0(g):
                done(pool, exp0, g)
                landed(pool, adj_landed, g)
                nc.gpsimd.tensor_tensor(E0[:, g.slot], E0[:, g.slot], adj_in[:, g.slot], ALU.mult).then_inc(E0_ready, 1)

            def times_adj1(g):
                done(pool, exp1, g)
                nc.gpsimd.tensor_tensor(E1[:, g.slot], E1[:, g.slot], adj_in[:, g.slot], ALU.mult).then_inc(E1_ready, 1)

            def std1(g):
                inverse_std(g, mv1, mv1_ready, var1, var1_ready, rstd1, rstd1_ready)

            def reduce_top():
                pool.wait_ge(top_ready, 1)
                nc.gpsimd.partition_all_reduce(top_all[:, :], top[:, :], P, bass.bass_isa.ReduceOp.max)\
                    .then_inc(top_reduced, 1)

            straight(((times_adj0, 0), (reduce_top, None), (times_adj0, 1), (std0, 0), (times_adj0, 2), (std0, 1),
                      (times_adj1, 0)))
            steady(pool, ((std0, 2), (times_adj0, 1), (times_adj1, 3), (std1, 4)))
            straight(((std0, -2), (times_adj0, -1), (times_adj1, -3), (std0, -1), (std1, -4), (times_adj1, -2),
                      (times_adj1, -1), (std1, -3), (std1, -2), (std1, -1)), B)

        @block.vector
        def _(dve):
            dve.wait_ge(ld_w, 16)
            dve.wait_ge(ld_a, 16)
            for c in range(C):
                last = nc.vector.tensor_tensor_reduce(product[:, c, :], w_a[:, c, 0:D], a_all[:, :], 1.0, 0.0, ALU.mult,
                                                      ALU.add, w_a[:, c, D:D + 1])
            last.then_inc(wa_ready, 1)

            steps = [0]

            def chained(instruction):
                steps[0] += 1
                instruction.then_inc(const_step, 1)
                dve.wait_ge(const_step, steps[0])

            def constant_products(i):
                for c in range(C):
                    nc.vector.tensor_tensor_reduce(product[:, C * (i + 1) + c, :], wv[:, c, :], aw_all[:, i, :],
                                                   1.0, 0.0, ALU.mult, ALU.add, v[:, c, i:i + 1])
                chained(nc.vector.tensor_tensor_reduce(product[:, 3 * C + i, :], bv_all[:, :], aw_all[:, i, :], 1.0,
                                                       0.0, ALU.mult, ALU.add, c_bias[:, i:i + 1]))

            def products_sj():
                dve.wait_ge(ld_const, 16 * 4)
                constant_products(0)

            def products_si():
                constant_products(1)

            def largest_entries():
                dve.wait_ge(ld_W, 16)
                for k in range(K):
                    nc.vector.tensor_reduce(top[:, k:k + 1], W[:, k], AX.XY, ALU.max, apply_absolute_value=True)
                nc.vector.tensor_reduce(top[:, K:K + 1], v[:, :, :], AX.XY, ALU.max, apply_absolute_value=True)\
                    .then_inc(top_ready, 1)

            def bias_of_s1():
                chained(nc.vector.tensor_tensor(c_bias[:, 2:3], c_bias[:, 0:1], c_bias[:, 1:2], ALU.add))
                nc.vector.memset(s1_bias[:, :, 0], 0.0)
                for t in range(T):
                    last = nc.vector.tensor_tensor(s1_bias[:, t, 1:2], c_bias[:, 2:3], ab_all[:, :], ALU.add)
                chained(last)

            def scales():
                dve.wait_ge(top_reduced, 1)
                chained(nc.vector.tensor_scalar(top[:, :], top_all[:, :], 1e-30, None, ALU.max))
                chained(nc.vector.tensor_scalar(power[:, :].bitcast(U32), top[:, :].bitcast(U32), EXPONENT, None,
                                                ALU.bitwise_and))
                chained(nc.vector.reciprocal(inv_power[:, :], power[:, :]))
                nc.vector.tensor_scalar(up[:, :], inv_power[:, :], W_TOP, None, ALU.mult).then_inc(up_ready, 1)
                chained(nc.vector.tensor_scalar(down[:, :], power[:, :], 1.0 / (W_TOP * X_SCALE), None, ALU.mult))

            def low_parts(parts):
                for src, k, lo, hi in parts:
                    last = nc.vector.scalar_tensor_tensor(out=Wl[:, :, lo:hi], in0=src, scalar=up[:, k:k + 1],
                                                          in1=Wh[:, :, lo:hi], op0=ALU.mult, op1=ALU.subtract)
                last.then_inc(W_ready, 1)

            def low_W2():
                dve.wait_ge(up_ready, 1)
                dve.wait_ge(Wh_ready, 1)
                low_parts(weight_parts[:2])

            def low_W10():
                dve.wait_ge(Wh_ready, 2)
                low_parts(weight_parts[2:])
                dve.wait_ge(b_sum_step, 2)

            def residual0_first(g):
                residual0(g, first_bank(g))

            def residual0(g, bank=pY):
                done(dve, attended0, g)
                nc.vector.reciprocal(inv0[:, g.slot], bank[:, :, D]).then_inc(inv0_ready, 1)
                done(dve, inv0_ready, g)
                done(dve, adj_summed, g)
                nc.vector.tensor_tensor(r0[:, g.slot], adj_sum[:, g.slot], inv0[:, g.slot], ALU.mult)\
                    .then_inc(r0_ready, 1)
                done(dve, r0_ready, g)
                landed(dve, x_landed, g)
                for t in range(T):
                    last = nc.vector.scalar_tensor_tensor(out=X1[:, g.slot, t, :], in0=bank[:, t, 0:D],
                                                          scalar=r0[:, g.slot, t:t + 1], in1=x_in[:, g.slot, t, :],
                                                          op0=ALU.mult, op1=ALU.add)
                last.then_inc(h_ready, 1)

            def stats0(g):
                done(dve, h_ready, g)
                statistics(g, X1, bn0, bn0_ready)

            def moments0(g):
                moments(g, bn0, bn0_ready, mv0, mv0_ready, waiter0)

            def statistics(g, rows, bn, bn_ready):
                for t in range(T):
                    last = nc.vector.bn_stats(bn[:, g.slot, t, :], rows[:, g.slot, t, :])
                last.then_inc(bn_ready, 1)

            def moments(g, bn, bn_ready, mv, mv_ready, waiter):
                done(dve, bn_ready, g)
                nc.vector.memset(waiter[:, g.slot], 0.0)
                for t in range(T):
                    last = nc.vector.bn_aggr(mv[:, g.slot, t, :], bn[:, g.slot, t, :])
                last.then_inc(mv_ready, 1)

            def add_V1(g):
                done(dve, hopped1, g)
                nc.vector.tensor_scalar(den1[:, g.slot], pX[:, :, D], 1e-12, None, ALU.add).then_inc(den1_ready, 1)
                done(dve, den1_ready, g)
                nc.vector.reciprocal(r1[:, g.slot], den1[:, g.slot]).then_inc(r1_ready, 1)
                done(dve, r1_ready, g)
                done(dve, V1_kept, g)
                for t in range(T):
                    last = nc.vector.scalar_tensor_tensor(out=U[:, g.slot, t, :], in0=pX[:, t, 0:D],
                                                          scalar=r1[:, g.slot, t:t + 1], in1=V1[:, g.slot, t, :],
                                                          op0=ALU.mult, op1=ALU.add)
                last.then_inc(U_ready, 1)

            def norm0(g):
                done(dve, rstd0_ready, g)
                for t in range(T):
                    last = nc.vector.tensor_scalar(X1[:, g.slot, t, :], X1[:, g.slot, t, :], mv0[:, g.slot, t, 0:1],
                                                   rstd0[:, g.slot, t:t + 1], ALU.subtract, ALU.mult)
                last.then_inc(X1_ready, 1)

            def leaky0(g):
                done(dve, tanh0, g)
                nc.vector.scalar_tensor_tensor(out=E0[:, g.slot], in0=E0[:, g.slot], scalar=0.1, in1=E0[:, g.slot],
                                               op0=ALU.mult, op1=ALU.max).then_inc(lrelu0, 1)

            def leaky1(g):
                done(dve, z1, g)
                nc.vector.scalar_tensor_tensor(out=E1[:, g.slot], in0=E1[:, g.slot], scalar=0.2, in1=E1[:, g.slot],
                                               op0=ALU.mult, op1=ALU.max).then_inc(lrelu1, 1)

            def low(g):
                done(dve, high_ready, g)
                nc.vector.scalar_tensor_tensor(out=Xhl[:, g.half, 1], in0=X1[:, g.slot], scalar=X_SCALE,
                                               in1=Xhl[:, g.half, 0], op0=ALU.mult, op1=ALU.subtract)\
                    .then_inc(low_ready, 1)

            def keep_V0(g):
                done(dve, weighed0, g)
                nc.vector.scalar_tensor_tensor(out=V0[:, g.slot], in0=p0[:, :, :], scalar=down[:, 0:1],
                                               in1=b_sum[:, None, :].to_broadcast([P, T, D]),
                                               op0=ALU.mult, op1=ALU.add).then_inc(V0_kept, 1)

            def residual1_last(g):
                residual1(g, p1)

            def residual1(g, bank=pU):
                done(dve, hopped2, g)
                done(dve, V0_kept, g)
                for t in range(T):
                    last = nc.vector.scalar_tensor_tensor(out=H[:, g.slot, t, :], in0=bank[:, t, :],
                                                          scalar=r1[:, g.slot, t:t + 1], in1=V0[:, g.slot, t, :],
                                                          op0=ALU.mult, op1=ALU.add)
                last.then_inc(H_ready, 1)

            def relu_add(g):
                done(dve, H_ready, g)
                nc.vector.scalar_tensor_tensor(out=H[:, g.slot], in0=H[:, g.slot], scalar=0.0, in1=X1[:, g.slot],
                                               op0=ALU.max, op1=ALU.add).then_inc(relu_added, 1)

            def stats1(g):
                done(dve, relu_added, g)
                statistics(g, H, bn1, bn1_ready)

            def moments1(g):
                moments(g, bn1, bn1_ready, mv1, mv1_ready, waiter1)

            def shift(g):
                done(dve, rstd1_ready, g)
                nc.vector.scalar_tensor_tensor(out=shift1[:, g.slot], in0=mv1[:, g.slot, :, 0], scalar=-1.0,
                                               in1=rstd1[:, g.slot], op0=ALU.mult, op1=ALU.mult)\
                    .then_inc(shift_ready, 1)

            def finish_last(g):
                done(dve, rstd1_ready, g)
                landed(dve, stored, g, 1)
                for t in range(T):
                    last = nc.vector.tensor_scalar(res[:, g.slot, t, :], H[:, g.slot, t, :], mv1[:, g.slot, t, 0:1],
                                                   rstd1[:, g.slot, t:t + 1], ALU.subtract, ALU.mult)
                last.then_inc(last_res_ready, 1)

            def s0_column(g):
                done(dve, embedded, g)
                nc.vector.tensor_scalar(s0[:, g.slot], first_bank(g)[:, :, D], 0.125, None, ALU.mult)\
                    .then_inc(s0_ready, 1)

            def s1_columns(g):
                done(dve, weighed2, g)
                nc.vector.scalar_tensor_tensor(out=s1[:, g.slot].rearrange("p k t -> p t k"), in0=pX[:, :, D:D + 2],
                                               scalar=down[:, 3:4], in1=s1_bias[:, :, :],
                                               op0=ALU.mult, op1=ALU.add).then_inc(s1_ready, 1)

            def make_diagonal(key, column):
                n, _ = spread_rows[key]
                dve.wait_ge(id_step, 7)
                for t in range(T):
                    last = nc.vector.tensor_scalar(diagonal[:, n, t, :], identity32[:, :], column[:, t:t + 1], None,
                                                   ALU.mult)
                last.then_inc(diagonal_ready, 1)

            def diagonal_s0(g):
                done(dve, s0_ready, g)
                make_diagonal(("s0", g.number), s0[:, g.slot])

            def diagonal_s1(g):
                done(dve, s1_ready, g)
                make_diagonal(("s1", g.number), s1[:, g.slot, 1])

            straight(((products_sj, None), (s0_column, 0), (diagonal_s0, 0), (s0_column, 1), (products_si, None),
                      (diagonal_s0, 1), (leaky0, 0), (s0_column, 2), (diagonal_s0, 2),
                      (largest_entries, None), (leaky0, 1), (s0_column, 3), (scales, None),
                      (bias_of_s1, None), (residual0_first, 0), (stats0, 0), (leaky0, 2),
                      (moments0, 0), (residual0_first, 1), (norm0, 0), (stats0, 1), (low, 0),
                      (moments0, 1), (low_W2, None), (norm0, 1), (low_W10, None), (low, 1),
                      (s1_columns, 0), (diagonal_s1, 0), (keep_V0, 0), (leaky1, 0),
                      (s1_columns, 1)))
            steady(dve, ((residual0, 2), (stats0, 2), (moments0, 2), (add_V1, 4), (norm0, 2), (leaky0, 1), (low, 2),
                         (leaky1, 3), (keep_V0, 3), (residual1, 4), (s0_column, 0), (relu_add, 4), (stats1, 4),
                         (s1_columns, 2), (moments1, 4), (shift, 4)))
            straight(((residual0, -2), (stats0, -2), (moments0, -2), (add_V1, -4), (norm0, -2), (leaky0, -1),
                      (low, -2), (residual1, -4), (keep_V0, -3), (leaky1, -3),
                      (residual0, -1), (s1_columns, -2), (stats0, -1), (moments0, -1),
                      (relu_add, -4), (diagonal_s1, -2), (norm0, -1), (stats1, -4), (low, -1),
                      (moments1, -4), (add_V1, -3), (keep_V0, -2), (shift, -4), (leaky1, -2),
                      (s1_columns, -1), (diagonal_s1, -1), (leaky1, -1), (residual1, -3),
                      (add_V1, -2), (relu_add, -3), (stats1, -3), (keep_V0, -1), (add_V1, -1),
                      (moments1, -3), (residual1, -2), (shift, -3), (relu_add, -2),
                      (stats1, -2), (residual1_last, -1), (moments1, -2), (relu_add, -1),
                      (stats1, -1), (shift, -2), (moments1, -1), (finish_last, -1)), B)


_ORDER = ["x", "xT", "adj", "adjT", "w", "a", "Wv", "bv", "aw", "ab", "Wk", "bk"]


def kernel(x, adj, L0_gnn_w, L0_gnn_a, L1_gnn_Wv, L1_gnn_bv, L1_gnn_aw, L1_gnn_ab, L1_gnn_Wk, L1_gnn_bk):
    import concourse.bacc as bacc
    from concourse.bass_utils import run_bass_kernel_spmd

    x, adj = np.asarray(x), np.asarray(adj)
    inputs = {
        "x": x, "xT": x.transpose(0, 2, 1), "adj": adj, "adjT": adj.transpose(0, 2, 1), "w": L0_gnn_w, "a": L0_gnn_a,
        "Wv": L1_gnn_Wv, "bv": L1_gnn_bv, "aw": L1_gnn_aw, "ab": L1_gnn_ab, "Wk": L1_gnn_Wk, "bk": L1_gnn_bk,
    }
    nc = bacc.Bacc("TRN2", target_bir_lowering=False, num_devices=1)
    arrays, args = {}, []
    for name in _ORDER:
        array = np.ascontiguousarray(np.asarray(inputs[name]))
        arrays[f"in_{name}"] = array
        args.append(nc.dram_tensor(f"in_{name}", array.shape, mybir.dt.from_np(array.dtype), kind="ExternalInput").ap())
    result = nc.dram_tensor("result", x.shape, F32, kind="ExternalOutput").ap()
    graph_layers_kernel(nc, *args, result)
    run = run_bass_kernel_spmd(nc, [arrays], core_ids=[0])
    return run.results[0]["result"]
```
